# Optimizing a Trainium2 kernel written in Bass

```python
import numpy as np
import jax
import jax.numpy as jnp

def _softmax(x, axis=-1):
    return jax.nn.softmax(x, axis=axis)

def _gelu(x):
    return jax.nn.gelu(x, approximate=True)

def _silu(x):
    return jax.nn.silu(x)

def _sigmoid(x):
    return jax.nn.sigmoid(x)

def _layernorm(x, axis=-1, eps=1e-05):
    m = jnp.mean(x, axis=axis, keepdims=True)
    v = jnp.var(x, axis=axis, keepdims=True)
    return (x - m) / jnp.sqrt(v + eps)

def _scatter_add(tgt, idx, src, axis=0):
    return tgt.at[idx].add(src)

def _segment_sum(src, seg, n):
    return jax.ops.segment_sum(src, seg, n)
kernel_name = 'mk_cond_seq_d2_seqx_r2_1871d7'

def setup_inputs(seed: int=0):
    np.random.seed(seed)
    _w = jnp.asarray

    def _rec_inputs():
        import jax
        import jax.numpy as jnp
        _rk = jax.random.key(seed)
        x = 1.648e-05 + 1 * jax.random.normal(jax.random.fold_in(_rk, 1), (8, 512, 576), jnp.float32)
        _lenS = 512 - jax.random.randint(jax.random.fold_in(_rk, 7), (8,), 0, max(1, 512 // 4) + 1, jnp.int32)
        _lenS2 = 512 - jax.random.randint(jax.random.fold_in(_rk, 8), (8,), 0, max(1, 512 // 4) + 1, jnp.int32)
        cond_1152 = 0.00914911 + 1.00357 * jax.random.normal(jax.random.fold_in(_rk, 11), (8, 576), jnp.float32)
        return (x, cond_1152)
    x, cond_1152 = _rec_inputs()

    def _L0_cond_setup():
        import jax, jax.numpy as jnp
        import numpy as np
        B, L, C = (8, 512, 576)
        H = 16
        D = C // H
        FF = int(C * 4.0)
        EPS = 1e-06

        def _layernorm(x):
            mu = jnp.mean(x, axis=-1, keepdims=True)
            var = jnp.mean(jnp.square(x - mu), axis=-1, keepdims=True)
            return (x - mu) * jax.lax.rsqrt(var + EPS)

        def _modulate(x, shift, scale):
            return x * (1.0 + scale) + shift

        def _attention(h, W_qkv, b_qkv, W_proj, b_proj):
            b, l, c = h.shape
            qkv = h @ W_qkv + b_qkv
            qkv = qkv.reshape(b, l, 3, H, D)
            q, k, v = (qkv[:, :, 0], qkv[:, :, 1], qkv[:, :, 2])
            scale = D ** (-0.5)
            scores = jnp.einsum('blhd,bmhd->bhlm', q * scale, k)
            attn = jax.nn.softmax(scores, axis=-1)
            o = jnp.einsum('bhlm,bmhd->blhd', attn, v).reshape(b, l, c)
            return o @ W_proj + b_proj
        key = jax.random.key(seed)
        ks = jax.random.split(key, 12)
        s = 0.02
        return {'x': jax.random.normal(ks[0], (B, L, C), jnp.float32), 'c': jax.random.normal(ks[1], (B, 1, C), jnp.float32), 'W_qkv': jax.random.normal(ks[2], (C, 3 * C), jnp.float32) * s, 'b_qkv': jnp.zeros((3 * C,), jnp.float32), 'W_proj': jax.random.normal(ks[3], (C, C), jnp.float32) * s, 'b_proj': jnp.zeros((C,), jnp.float32), 'W_fc1': jax.random.normal(ks[4], (C, FF), jnp.float32) * s, 'b_fc1': jnp.zeros((FF,), jnp.float32), 'W_fc2': jax.random.normal(ks[5], (FF, C), jnp.float32) * s, 'b_fc2': jnp.zeros((C,), jnp.float32), 'W_ada': jax.random.normal(ks[6], (C, 6 * C), jnp.float32) * s, 'b_ada': jnp.zeros((6 * C,), jnp.float32)}
    _L0_cond_all = _L0_cond_setup()
    _L0_cond_in = {k: v for k, v in _L0_cond_all.items() if k in ('W_qkv', 'b_qkv', 'W_proj', 'b_proj', 'W_fc1', 'b_fc1', 'W_fc2', 'b_fc2', 'W_ada', 'b_ada')}
    del _L0_cond_all

    def _L1_cond_setup():
        import jax, jax.numpy as jnp
        import numpy as np
        from jax.scipy.linalg import expm
        N, D, COND_DIM = (576, 64, 576)
        B, T = (16, 512)

        def _rotation(cond, W, b):
            v = jax.nn.silu(cond) @ W.T + b
            iu, ju = jnp.triu_indices(D, k=1)
            A = jnp.zeros((cond.shape[0], D, D), dtype=v.dtype)
            A = A.at[:, iu, ju].set(v).at[:, ju, iu].set(-v)
            return expm(A)
        key = jax.random.key(seed)
        k1, k2, k3, k4, k5 = jax.random.split(key, 5)
        x = jax.random.normal(k1, (B, T, N), dtype=jnp.float32)
        cond = jax.random.normal(k2, (B, COND_DIM), dtype=jnp.float32)
        P = jax.random.normal(k3, (N, D), dtype=jnp.float32)
        n_skew = D * (D - 1) // 2
        bound = 1.0 / np.sqrt(COND_DIM)
        W = jax.random.uniform(k4, (n_skew, COND_DIM), minval=-bound, maxval=bound, dtype=jnp.float32)
        b = jax.random.uniform(k5, (n_skew,), minval=-bound, maxval=bound, dtype=jnp.float32)
        return {'x': x, 'cond': cond, 'P': P, 'W': W, 'b': b}
    _L1_cond_all = _L1_cond_setup()
    _L1_cond_in = {k: v for k, v in _L1_cond_all.items() if k in ('P', 'W', 'b')}
    del _L1_cond_all
    return {'x': x, 'cond_1152': cond_1152, 'L0_cond_W_qkv': _L0_cond_in['W_qkv'], 'L0_cond_b_qkv': _L0_cond_in['b_qkv'], 'L0_cond_W_proj': _L0_cond_in['W_proj'], 'L0_cond_b_proj': _L0_cond_in['b_proj'], 'L0_cond_W_fc1': _L0_cond_in['W_fc1'], 'L0_cond_b_fc1': _L0_cond_in['b_fc1'], 'L0_cond_W_fc2': _L0_cond_in['W_fc2'], 'L0_cond_b_fc2': _L0_cond_in['b_fc2'], 'L0_cond_W_ada': _L0_cond_in['W_ada'], 'L0_cond_b_ada': _L0_cond_in['b_ada'], 'L1_cond_P': _L1_cond_in['P'], 'L1_cond_W': _L1_cond_in['W'], 'L1_cond_b': _L1_cond_in['b']}

def reference(x, cond_1152, L0_cond_W_qkv, L0_cond_b_qkv, L0_cond_W_proj, L0_cond_b_proj, L0_cond_W_fc1, L0_cond_b_fc1, L0_cond_W_fc2, L0_cond_b_fc2, L0_cond_W_ada, L0_cond_b_ada, L1_cond_P, L1_cond_W, L1_cond_b):
    import jax
    import jax.numpy as jnp

    def _L0_cond_ref(x, c, W_qkv, b_qkv, W_proj, b_proj, W_fc1, b_fc1, W_fc2, b_fc2, W_ada, b_ada):
        import jax, jax.numpy as jnp
        import numpy as np
        B, L, C = (8, 512, 576)
        H = 16
        D = C // H
        FF = int(C * 4.0)
        EPS = 1e-06

        def _layernorm(x):
            mu = jnp.mean(x, axis=-1, keepdims=True)
            var = jnp.mean(jnp.square(x - mu), axis=-1, keepdims=True)
            return (x - mu) * jax.lax.rsqrt(var + EPS)

        def _modulate(x, shift, scale):
            return x * (1.0 + scale) + shift

        def _attention(h, W_qkv, b_qkv, W_proj, b_proj):
            b, l, c = h.shape
            qkv = h @ W_qkv + b_qkv
            qkv = qkv.reshape(b, l, 3, H, D)
            q, k, v = (qkv[:, :, 0], qkv[:, :, 1], qkv[:, :, 2])
            scale = D ** (-0.5)
            scores = jnp.einsum('blhd,bmhd->bhlm', q * scale, k)
            attn = jax.nn.softmax(scores, axis=-1)
            o = jnp.einsum('bhlm,bmhd->blhd', attn, v).reshape(b, l, c)
            return o @ W_proj + b_proj
        ada = jax.nn.silu(c) @ W_ada + b_ada
        shift_msa, scale_msa, gate_msa, shift_mlp, scale_mlp, gate_mlp = jnp.split(ada, 6, axis=-1)
        h = _modulate(_layernorm(x), shift_msa, scale_msa)
        x = x + gate_msa * _attention(h, W_qkv, b_qkv, W_proj, b_proj)
        h = _modulate(_layernorm(x), shift_mlp, scale_mlp)
        mlp = jax.nn.gelu(h @ W_fc1 + b_fc1, approximate=True) @ W_fc2 + b_fc2
        x = x + gate_mlp * mlp
        return x

    def _L1_cond_ref(x, cond, P, W, b):
        import jax, jax.numpy as jnp
        import numpy as np
        from jax.scipy.linalg import expm
        N, D, COND_DIM = (576, 64, 576)
        B, T = (16, 512)

        def _rotation(cond, W, b):
            v = jax.nn.silu(cond) @ W.T + b
            iu, ju = jnp.triu_indices(D, k=1)
            A = jnp.zeros((cond.shape[0], D, D), dtype=v.dtype)
            A = A.at[:, iu, ju].set(v).at[:, ju, iu].set(-v)
            return expm(A)
        U, _ = jnp.linalg.qr(P)
        R = _rotation(cond, W, b)
        z = jnp.einsum('btn,nd->btd', x, U)
        z_rot = jnp.einsum('btd,bde->bte', z, R)
        x_rot = x + jnp.einsum('btd,nd->btn', z_rot - z, U)
        return x_rot
    x = _L0_cond_ref(x, cond_1152[:, None, :], L0_cond_W_qkv, L0_cond_b_qkv, L0_cond_W_proj, L0_cond_b_proj, L0_cond_W_fc1, L0_cond_b_fc1, L0_cond_W_fc2, L0_cond_b_fc2, L0_cond_W_ada, L0_cond_b_ada)
    x = _L1_cond_ref(x, cond_1152, L1_cond_P, L1_cond_W, L1_cond_b)
    return x

_drawn_inputs = setup_inputs


def setup_inputs(seed=0):
    import zlib

    import numpy as np

    out = dict(_drawn_inputs(seed))
    spreads = {'L0_cond_b_qkv': (0.0, 0.594),
     'L0_cond_b_proj': (0.0, 0.1),
     'L0_cond_b_fc1': (0.0, 0.44),
     'L0_cond_b_fc2': (0.0, 0.273),
     'L0_cond_b_ada': (0.0, 0.1)}
    factors = {}
    for name, (base, spread) in spreads.items():
        noise = np.random.default_rng([zlib.crc32(name.encode()), seed]).standard_normal(out[name].shape)
        drawn = base * np.exp(spread * noise) if base else spread * noise
        out[name] = jnp.asarray(drawn.astype(out[name].dtype))
    for name, factor in factors.items():
        out[name] = (out[name] * factor).astype(out[name].dtype)
    return out
```

```python
import concourse.bass as bass
import numpy as np
from concourse import mybir
from contextlib import ExitStack

BATCH, TOKENS, C = 8, 512, 576
HEADS = 16
HD = C // HEADS
FF = 4 * C
RANK = 64
PAR = 128
KT = 4
REM = C - KT * PAR
HALF = C // 2
TT = TOKENS // PAR
LN_EPS = 1e-6
SCALE = float(HD) ** -0.5

SQUARINGS = 16
TAYLOR = [1.0]
for _n in range(1, 13):
    TAYLOR.append(TAYLOR[-1] / _n)

W_PARTS, A_PARTS = 2 * KT + 1, 2 * KT + 2
PASSES = []
for _t in range(KT):
    PASSES += [(_t, _t, PAR), (_t, KT + _t, PAR), (KT + _t, _t, PAR)]
PASSES += [(2 * KT, 2 * KT, PAR), (2 * KT, 2 * KT + 1, REM)]

QK_COLS = 2 * C
QK_TILES = QK_COLS // PAR
RING = 4
STACK = 3 * HD
MROW = STACK


def pieces(t):
    out = []
    col = t * PAR
    while col < (t + 1) * PAR:
        block, row = divmod(col, HD)
        n = min(HD - row, (t + 1) * PAR - col)
        out.append((block // 2, block % 2, row, n, col - t * PAR))
        col += n
    return out


MOVES = {(s, p): 0 for s in range(RING) for p in range(2)}
MOVES_AFTER = []
for _t in range(QK_TILES):
    for _h, _k, _r, _n, _p in pieces(_t):
        MOVES[_h % RING, _t % 2] += 3
    MOVES_AFTER.append(dict(MOVES))


def last_tile(h):
    return -(-2 * HD * (h + 1) // PAR) - 1


def build(nc, x, cond_t, w_ada, b_ada, w_qk, b_qk, w_v, b_v, w_proj, b_proj, w_fc1, b_fc1, w_fc2,
          b_fc2, p_cols, p_rows, w_rot, b_rot, ada_d, x1_d, rot_d, e_d, out):
    fp32, fp32r = mybir.dt.float32, mybir.dt.float32r
    ALU, ACT, AX = mybir.AluOpType, mybir.ActivationFunctionType, mybir.AxisListType
    ADD_ALL = bass.bass_isa.ReduceOp.add
    every = ExitStack()

    def sem(name):
        return every.enter_context(nc.semaphore(name))

    def sb(ctx, name, shape, dt=fp32):
        return ctx.enter_context(nc.sbuf_tensor(name, shape, dt))

    def f32(ap):
        return ap.bitcast(fp32)

    def alone(engine):
        engine.nop(nofuse=True)

    with every:
        PB = [every.enter_context(nc.psum_tensor(f"bank{i}", [PAR, 512], fp32)) for i in range(8)]
        ident = sb(every, "ident", [PAR, PAR])
        adaT = sb(every, "adaT", [PAR, 4, KT + 1, BATCH])
        siluT = sb(every, "siluT", [PAR, KT + 1, BATCH])
        chol = sb(every, "chol", [RANK, 3 * RANK])
        lu = sb(every, "lu", [RANK, RANK])
        dcol = sb(every, "dcol", [RANK, 1])
        scol = sb(every, "scol", [RANK, 1])
        invroot = sb(every, "invroot", [RANK, 1])
        below = sb(every, "below", [RANK, RANK])

        const_ready = sem("const_ready")
        cond_in, bada_in, ada_in0, ada_in1 = sem("cond_in"), sem("bada_in"), sem("ada_in0"), sem("ada_in1")
        ada_in = [ada_in0, ada_in1]
        silu_done, ada_mm, ada_rows, ada_stored = sem("silu_done"), sem("ada_mm"), sem("ada_rows"), sem("ada_stored")
        adaT_mm, adaT_done = sem("adaT_mm"), sem("adaT_done")
        stage_in = [sem(f"stage_in{i}") for i in range(3)]
        hi_done, lo_done, beff_step = sem("hi_done"), sem("lo_done"), sem("beff_step")
        bvec_in, bvb_done, beff_done = sem("bvec_in"), sem("bvb_done"), sem("beff_done")
        p_in, g_mm, chol_init = sem("p_in"), sem("g_mm"), sem("chol_init")

        attn = ExitStack()
        every.enter_context(attn)
        wqk = sb(attn, "wqk", [PAR, W_PARTS, QK_COLS], fp32r)
        wv = sb(attn, "wv", [PAR, W_PARTS, C], fp32r)
        wp = sb(attn, "wp", [PAR, W_PARTS, C], fp32r)
        beff = sb(attn, "beff", [PAR, C])
        bqk = sb(attn, "bqk", [PAR, QK_TILES])
        stages = ExitStack()
        cond = sb(stages, "cond", [PAR, KT + 1, BATCH])
        bada = sb(stages, "bada", [BATCH, 6 * C])
        ada = sb(stages, "ada", [BATCH, 6 * C])
        wada = [sb(stages, f"wada{i}", [PAR, KT + 1, 512]) for i in range(2)]
        stage = [sb(stages, f"stage{i}", [PAR, QK_COLS]) for i in range(3)]
        bv = sb(stages, "bv", [PAR, KT + 1])
        bproj = sb(stages, "bproj", [PAR, C])
        bvb = sb(stages, "bvb", [PAR, KT + 1, PAR])
        pcol = sb(stages, "pcol", [PAR, KT + 1, RANK])
        ptop = sb(stages, "ptop", [RANK, RANK])

        ADA_CHUNKS = [(i, min(512, 6 * C - i)) for i in range(0, 6 * C, 512)]
        SPLITS = [(w_proj, wp, C), (w_qk, wqk, QK_COLS), (w_v, wv, C)]
        STAGES = [(src, dst, n, t) for src, dst, n in SPLITS for t in range(KT + 1)]

        with nc.Block() as block:
            @block.sync
            def _(sp):
                sp.dma_start(cond[:, :, :], cond_t.rearrange("k p b -> p k b")).then_inc(cond_in, 16)
                sp.dma_start(bada[:, :], b_ada.partition_broadcast(BATCH)).then_inc(bada_in, 16)
                sp.dma_start(bv[:, :], b_v).then_inc(bvec_in, 16)
                sp.dma_start(bqk[:, :], b_qk).then_inc(bvec_in, 16)
                sp.dma_start(bproj[:, :], b_proj.partition_broadcast(PAR)).then_inc(bvec_in, 16)
                sp.dma_start(pcol[:, 0:KT, :], p_cols[0:KT * PAR, :].rearrange("(k p) d -> p k d", p=PAR)).then_inc(p_in, 16)
                sp.dma_start(pcol[0:REM, KT, :], p_cols[KT * PAR:C, :]).then_inc(p_in, 16)
                sp.dma_start(ptop[:, :], p_rows[:, 0:RANK]).then_inc(p_in, 16)
                for i, (c0, n) in enumerate(ADA_CHUNKS):
                    if i >= 2:
                        sp.wait_ge(ada_mm, i - 1)
                    sp.dma_start(wada[i % 2][:, 0:KT, 0:n], w_ada[0:KT * PAR, c0:c0 + n].rearrange("(k p) n -> p k n", p=PAR)).then_inc(ada_in[i % 2], 16)
                    sp.dma_start(wada[i % 2][0:REM, KT, 0:n], w_ada[KT * PAR:C, c0:c0 + n]).then_inc(ada_in[i % 2], 16)
                for i, (src, dst, n, t) in enumerate(STAGES):
                    if i >= 3:
                        sp.wait_ge(lo_done, i - 2)
                        if i - 3 <= KT:
                            sp.wait_ge(beff_step, i - 2)
                    rows = PAR if t < KT else REM
                    sp.dma_start(stage[i % 3][0:rows, 0:n], src[t * PAR:t * PAR + rows, :]).then_inc(stage_in[i % 3], 16)
                sp.wait_ge(ada_rows, len(ADA_CHUNKS))
                sp.dma_start(ada_d, ada[:, :]).then_inc(ada_stored, 16)
                sp.wait_ge(ada_stored, 16)

            @block.gpsimd
            def _(pool):
                pool.memset(ident[:, :], 0.0).then_inc(const_ready, 1)
                pool.memset(below[:, :], 0.0).then_inc(const_ready, 1)
                pool.memset(dcol[:, :], 0.0).then_inc(const_ready, 1)
                pool.memset(scol[:, :], 0.0).then_inc(const_ready, 1)
                pool.wait_ge(const_ready, 4)
                pool.affine_select(out=ident[:, :], in_=ident[:, :], compare_op=ALU.not_equal, fill=1.0, base=0,
                                   pattern=[[-1, PAR]], channel_multiplier=1).then_inc(const_ready, 1)
                pool.affine_select(out=below[:, :], in_=below[:, :], compare_op=ALU.is_ge, fill=-1.0, base=0,
                                   pattern=[[1, RANK]], channel_multiplier=-1).then_inc(const_ready, 1)

            @block.scalar
            def _(act):
                act.wait_ge(cond_in, 16)
                act.activation(siluT[:, :, :], cond[:, :, :], ACT.Silu).then_inc(silu_done, 1)
                for i, (src, dst, n, t) in enumerate(STAGES):
                    rows = PAR if t < KT else REM
                    act.wait_ge(stage_in[i % 3], 16 * (i // 3 + 1))
                    act.activation(dst[0:rows, t if t < KT else 2 * KT, :], stage[i % 3][0:rows, 0:n], ACT.Copy).then_inc(hi_done, 1)

            @block.vector
            def _(dve):
                dve.wait_ge(bvec_in, 48)
                dve.memset(bvb[:, :, :], 1.0).then_inc(bvb_done, 1)
                dve.wait_ge(bvb_done, 1)
                for t in range(KT + 1):
                    dve.tensor_scalar(bvb[:, t, :], bvb[:, t, :], bv[:, t:t + 1], None, ALU.mult).then_inc(bvb_done, 1)
                dve.wait_ge(g_mm, 1)
                dve.wait_ge(const_ready, 6)
                dve.tensor_copy(chol[:, 0:RANK], PB[5][0:RANK, 0:RANK]).then_inc(chol_init, 1)
                dve.tensor_copy(chol[:, RANK:2 * RANK], ident[0:RANK, 0:RANK]).then_inc(chol_init, 1)
                dve.tensor_copy(chol[:, 2 * RANK:3 * RANK], ptop[:, :]).then_inc(chol_init, 1)
                dve.wait_ge(bada_in, 16)
                for i, (c0, n) in enumerate(ADA_CHUNKS):
                    dve.wait_ge(ada_mm, i + 1)
                    dve.tensor_tensor(ada[:, c0:c0 + n], PB[i % 2][0:BATCH, 0:n], bada[:, c0:c0 + n], ALU.add).then_inc(ada_rows, 1)
                dve.wait_ge(adaT_mm, 1)
                for j in range(4):
                    for rows, f0, f1 in ((PAR, 0, KT), (REM, KT, KT + 1)):
                        dve.tensor_scalar(adaT[0:rows, j, f0:f1, :],
                                          PB[4][0:rows, 40 * j + 8 * f0:40 * j + 8 * f1].rearrange("p (f b) -> p f b", b=BATCH),
                                          float(j % 2), None, ALU.add).then_inc(adaT_done, 1)
                for i, (src, dst, n, t) in enumerate(STAGES):
                    dve.wait_ge(hi_done, i + 1)
                    if t < KT:
                        dve.tensor_tensor(dst[:, KT + t, :], stage[i % 3][:, 0:n], f32(dst[:, t, :]), ALU.subtract).then_inc(lo_done, 1)
                    else:
                        dve.tensor_tensor(dst[REM:PAR, 2 * KT, :], stage[i % 3][0:REM, 0:n], f32(dst[0:REM, 2 * KT, :]), ALU.subtract).then_inc(lo_done, 1)
                    if i == KT:
                        dve.wait_ge(beff_step, KT + 1)
                        for half in range(2):
                            dve.tensor_tensor(beff[:, half * HALF:(half + 1) * HALF], PB[2 + half][:, 0:HALF],
                                              bproj[:, half * HALF:(half + 1) * HALF], ALU.add).then_inc(beff_done, 1)

            @block.tensor
            def _(pe):
                pe.wait_ge(p_in, 48)
                for t in range(KT + 1):
                    rows = PAR if t < KT else REM
                    mm = pe.matmul(PB[5][0:RANK, 0:RANK], pcol[0:rows, t, :], pcol[0:rows, t, :], start=(t == 0), stop=(t == KT))
                mm.then_inc(g_mm, 1)
                pe.wait_ge(silu_done, 1)
                for i, (c0, n) in enumerate(ADA_CHUNKS):
                    pe.wait_ge(ada_in[i % 2], 32 * (i // 2 + 1))
                    if i >= 2:
                        pe.wait_ge(ada_rows, i - 1)
                    for t in range(KT + 1):
                        rows = PAR if t < KT else REM
                        mm = pe.matmul(PB[i % 2][0:BATCH, 0:n], siluT[0:rows, t, :], wada[i % 2][0:rows, t, 0:n], start=(t == 0), stop=(t == KT))
                    mm.then_inc(ada_mm, 1)
                pe.wait_ge(ada_rows, len(ADA_CHUNKS))
                pe.wait_ge(const_ready, 6)
                for j, section in enumerate((0, 1, 3, 4)):
                    for f in range(KT + 1):
                        rows, c0 = (PAR if f < KT else REM), section * C + f * PAR
                        mm = pe.transpose(PB[4][0:rows, 40 * j + 8 * f:40 * j + 8 * f + 8], ada[:, c0:c0 + rows],
                                          ident[0:BATCH, 0:BATCH])
                mm.then_inc(adaT_mm, 1)
                pe.wait_ge(bvb_done, KT + 2)
                for t in range(KT + 1):
                    rows = PAR if t < KT else REM
                    pe.wait_ge(stage_in[t % 3], 16 * (t // 3 + 1))
                    for half in range(2):
                        mm = pe.matmul(PB[2 + half][:, 0:HALF], bvb[0:rows, t, :], stage[t % 3][0:rows, half * HALF:(half + 1) * HALF],
                                       start=(t == 0), stop=(t == KT))
                    mm.then_inc(beff_step, 1)
        stages.close()

        acts = ExitStack()
        xln = sb(acts, "xln", [PAR, TT, C])
        stats = sb(acts, "stats", [PAR, TT, 2, 6])
        mv = sb(acts, "mv", [PAR, TT, 2])
        rstd = sb(acts, "rstd", [PAR, 2, TT])
        mhalf = sb(acts, "mhalf", [PAR, TT])
        hf = [sb(acts, f"hf{i}", [PAR, TOKENS]) for i in range(2)]
        hT = sb(acts, "hT", [PAR, A_PARTS, TOKENS], fp32r)
        vv = sb(acts, "vv", [PAR, TT, HEADS, 2 * HD + 1], fp32r)
        qkhi = [sb(acts, f"qkhi{i}", [PAR, TOKENS], fp32r) for i in range(2)]
        qklo = [sb(acts, f"qklo{i}", [PAR, TOKENS], fp32r) for i in range(2)]
        qs = [sb(acts, f"qs{i}", [MROW + 1, TOKENS], fp32r) for i in range(RING)]
        ks = [sb(acts, f"ks{i}", [MROW + 1, TOKENS], fp32r) for i in range(RING)]
        negm = [sb(acts, f"negm{i}", [PAR, TT]) for i in range(2)]
        mrow = [sb(acts, f"mrow{i}", [TT, PAR], fp32r) for i in range(2)]
        pf = [sb(acts, f"pf{i}", [PAR, TOKENS]) for i in range(2)]
        phi = [sb(acts, f"phi{i}", [PAR, TOKENS], fp32r) for i in range(2)]
        plo = [sb(acts, f"plo{i}", [PAR, TOKENS], fp32r) for i in range(2)]
        ots = [sb(acts, f"ots{i}", [2 * HD + 1, TOKENS]) for i in range(2)]
        recip = [sb(acts, f"recip{i}", [PAR, TT]) for i in range(2)]
        oo = sb(acts, "oo", [PAR, TT, C])
        aT = sb(acts, "aT", [PAR, A_PARTS, PAR], fp32r)
        gate = sb(acts, "gate", [PAR, C])
        gb = sb(acts, "gb", [PAR, C])
        xr = [sb(acts, f"xr{i}", [PAR, C]) for i in range(2)]
        xo = [sb(acts, f"xo{i}", [PAR, C]) for i in range(2)]

        masked = sb(acts, "masked", [RANK, 3 * RANK])
        prow = sb(acts, "prow", [RANK, 3 * RANK])
        small = sb(acts, "small", [RANK, 9])
        inv, factor, minus1, sign, placed, onehot, neg, column, pivot = (
            small[:, i:i + 1] for i in range(9))

        G, M, S, O, X = PB[0:2], PB[2:4], PB[4:6], PB[6], PB[7]
        OW = 2 * HD + 2
        G_LN, G_V, G_QK, G_P = 0, KT + 1, KT + 1 + 2 * TT, KT + 1 + 2 * TT + QK_TILES
        G_ALL = G_P + 4 * TT
        assert G_ALL % 2 == 0

        x_in, st_done, mv_done = sem("x_in"), sem("st_done"), sem("mv_done")
        rstd_step, ln_norm, hT_hi, hT_split = sem("rstd_step"), sem("ln_norm"), sem("hT_hi"), sem("hT_split")
        g_full, g_free = sem("g_full"), sem("g_free")
        v_hi = sem("v_hi")
        qk_hi = sem("qk_hi")
        moved = {(s, p): sem(f"moved{s}{p}") for s in range(RING) for p in range(2)}
        m_full, m_read, mT, mrow_done = sem("m_full"), sem("m_read"), sem("mT"), sem("mrow_done")
        mrow_in = [sem("mrow_in0"), sem("mrow_in1")]
        s_full, scored, exp_f, exp_hi, p_lo, pv = sem("s_full"), sem("scored"), sem("exp_f"), sem("exp_hi"), sem("p_lo"), sem("pv")
        ot_done, oT, recip_done, o_read, o_norm = sem("ot_done"), sem("oT"), sem("recip_done"), sem("o_read"), sem("o_norm")
        a_hi = sem("a_hi")
        gate_in, gb_done = sem("gate_in"), sem("gb_done")
        xr_in, xr_done, xo_done = [sem("xr_in0"), sem("xr_in1")], sem("xr_done"), sem("xo_done")
        x1_out = [sem("x1_out0"), sem("x1_out1")]
        fixed = sem("fixed")
        elim = sem("elim")

        xb = x.rearrange("b (t p) c -> b p t c", p=PAR)
        x1b = x1_d.rearrange("b (t p) c -> b p t c", p=PAR)

        def q_tiles_before(h):
            first = last_tile(h) + 1 if h else 0
            return range(first, last_tile(min(h + 1, HEADS - 1)) + 1)

        with nc.Block() as block:
            @block.sync
            def _(sp):
                sp.sem_inc(mrow_in[0], 16)
                sp.sem_inc(mrow_in[1], 16)
                sp.sem_inc(x1_out[0], 16)
                sp.sem_inc(x1_out[1], 16)
                for key in MOVES:
                    sp.sem_inc(moved[key], 16)
                sp.wait_ge(fixed, RING + 3)

                def batch(b):
                    def move_qk(t):
                        sp.wait_ge(g_free, b * G_ALL + G_QK + t + 3)
                        seen = set()
                        for h, is_k, r, n, p0 in pieces(t):
                            slot = h % RING
                            if h not in seen:
                                sp.wait_ge(scored, b * HEADS + h + 1)
                                seen.add(h)
                            hi, lo = qkhi[t % 2][p0:p0 + n, :], qklo[t % 2][p0:p0 + n, :]
                            dst = (ks if is_k else qs)[slot]
                            for j, part in enumerate((hi, hi, lo) if is_k else (hi, lo, hi)):
                                sp.dma_start(f32(dst[j * HD + r:j * HD + r + n, :]), f32(part)).then_inc(moved[slot, t % 2], 16)

                    def move_mrow(h):
                        sp.wait_ge(mrow_done, b * HEADS + h + 1)
                        sp.dma_start(f32(qs[h % RING][MROW:MROW + 1, :]), f32(mrow[h % 2][:, :])).then_inc(mrow_in[h % 2], 16)

                    def load_xr(qt):
                        sp.wait_ge(xo_done, b * TT + qt + 1)
                        sp.dma_start(xr[qt % 2][:, :].unsqueeze(1), xb[bass.ds(b, 1), :, qt, :].rearrange("o p c -> p o c")).then_inc(xr_in[qt % 2], 16)

                    sp.wait_ge(g_free, b * G_ALL + 2)
                    sp.dma_start(xln[:, :, :].unsqueeze(1), xb[bass.ds(b, 1)].rearrange("o p t c -> p o t c")).then_inc(x_in, 16)
                    sp.dma_start(gate[:, :], ada_d[bass.ds(b, 1), 2 * C:3 * C].partition_broadcast(PAR)).then_inc(gate_in, 16)
                    load_xr(0)
                    load_xr(1)
                    for h in range(HEADS):
                        for t in q_tiles_before(h):
                            move_qk(t)
                        if h == 0:
                            move_mrow(0)
                        if h + 1 < HEADS:
                            move_mrow(h + 1)
                    for qt in range(TT):
                        if qt >= 2:
                            load_xr(qt)
                        sp.wait_ge(xo_done, b * TT + qt + 3)
                        sp.dma_start(x1b[bass.ds(b, 1), :, qt, :].rearrange("o p c -> p o c"), xo[qt % 2][:, :].unsqueeze(1)).then_inc(x1_out[qt % 2], 16)

                for phase in range(2):
                    with sp.Fori(0, BATCH // 2) as i:
                        batch(i + phase * (BATCH // 2))
                for parity in range(2):
                    sp.wait_ge(x1_out[parity], 16 * (BATCH * TT // 2 + 1))

            @block.gpsimd
            def _(pool):
                pool.memset(mhalf[:, :], -0.5).then_inc(fixed, 1)
                pool.sem_inc(hT_split, 2)
                pool.sem_inc(xo_done, 2)
                pool.sem_inc(o_norm, 2)

                pool.memset(minus1[:, :], -1.0).then_inc(fixed, 1)
                pool.wait_ge(fixed, RING + 3)
                pool.sem_inc(elim, 1)
                CHOLESKY_OPS, LU_OPS, TURN_OPS = 10, 15, 2

                def cholesky_step(k):
                    base = k * CHOLESKY_OPS
                    pool.wait_ge(elim, base + 1)
                    alone(pool)
                    pool.tensor_copy(onehot[:, :], ident[0:RANK, bass.ds(k, 1)]).then_inc(elim, 1)
                    pool.tensor_copy(neg[:, :], below[:, bass.ds(k, 1)]).then_inc(elim, 1)
                    pool.tensor_copy(column[:, :], chol[:, bass.ds(k, 1)]).then_inc(elim, 1)
                    base = base + 3
                    pool.wait_ge(elim, base + 1)
                    alone(pool)
                    pool.tensor_scalar(masked[:, :], chol[:, :], onehot[:, :], None, ALU.mult).then_inc(elim, 1)
                    pool.wait_ge(elim, base + 2)
                    alone(pool)
                    pool.partition_all_reduce(prow[:, :], masked[:, :], RANK, ADD_ALL).then_inc(elim, 1)
                    pool.tensor_tensor(dcol[:, :], dcol[:, :], masked[:, bass.ds(k, 1)], ALU.add).then_inc(elim, 1)
                    pool.wait_ge(elim, base + 4)
                    alone(pool)
                    pool.tensor_tensor(inv[:, :], prow[:, bass.ds(k, 1)], minus1[:, :], ALU.pow).then_inc(elim, 1)
                    pool.wait_ge(elim, base + 5)
                    alone(pool)
                    pool.tensor_scalar(factor[:, :], column[:, :], inv[:, :], neg[:, :], ALU.mult, ALU.mult).then_inc(elim, 1)
                    pool.wait_ge(elim, base + 6)
                    alone(pool)
                    pool.tensor_scalar(masked[:, :], prow[:, :], factor[:, :], None, ALU.mult).then_inc(elim, 1)
                    pool.wait_ge(elim, base + 7)
                    pool.tensor_tensor(chol[:, :], chol[:, :], masked[:, :], ALU.add).then_inc(elim, 1)

                def turn_to_signs():
                    base = RANK * CHOLESKY_OPS
                    pool.wait_ge(elim, base + 1)
                    pool.tensor_tensor(invroot[:, :], dcol[:, :], mhalf[0:RANK, 0:1], ALU.pow).then_inc(elim, 1)
                    pool.wait_ge(elim, base + 2)
                    alone(pool)
                    pool.tensor_scalar(lu[:, :], chol[:, 2 * RANK:3 * RANK], invroot[:, :], None, ALU.mult).then_inc(elim, 1)

                def sign_step(k):
                    base = k * LU_OPS + RANK * CHOLESKY_OPS + TURN_OPS
                    rows = masked[:, 0:RANK]
                    pool.wait_ge(elim, base + 1)
                    alone(pool)
                    pool.tensor_copy(onehot[:, :], ident[0:RANK, bass.ds(k, 1)]).then_inc(elim, 1)
                    pool.tensor_copy(neg[:, :], below[:, bass.ds(k, 1)]).then_inc(elim, 1)
                    pool.tensor_copy(column[:, :], lu[:, bass.ds(k, 1)]).then_inc(elim, 1)
                    base = base + 3
                    pool.wait_ge(elim, base + 1)
                    alone(pool)
                    pool.tensor_scalar(rows, lu[:, :], onehot[:, :], None, ALU.mult).then_inc(elim, 1)
                    pool.wait_ge(elim, base + 2)
                    alone(pool)
                    pool.partition_all_reduce(prow[:, 0:RANK], rows, RANK, ADD_ALL).then_inc(elim, 1)
                    pool.wait_ge(elim, base + 3)
                    alone(pool)
                    pool.tensor_copy(pivot[:, :], prow[:, bass.ds(k, 1)]).then_inc(elim, 1)
                    base = base + 1
                    pool.wait_ge(elim, base + 3)
                    alone(pool)
                    pool.tensor_scalar(sign[:, :], pivot[:, :], 0.0, -2.0, ALU.is_ge, ALU.mult).then_inc(elim, 1)
                    pool.wait_ge(elim, base + 4)
                    alone(pool)
                    pool.tensor_scalar(sign[:, :], sign[:, :], 1.0, None, ALU.add).then_inc(elim, 1)
                    pool.wait_ge(elim, base + 5)
                    pool.tensor_tensor(inv[:, :], pivot[:, :], sign[:, :], ALU.subtract).then_inc(elim, 1)
                    pool.wait_ge(elim, base + 6)
                    pool.tensor_tensor(inv[:, :], inv[:, :], minus1[:, :], ALU.pow).then_inc(elim, 1)
                    pool.tensor_tensor(placed[:, :], onehot[:, :], sign[:, :], ALU.mult).then_inc(elim, 1)
                    pool.wait_ge(elim, base + 8)
                    pool.tensor_tensor(scol[:, :], scol[:, :], placed[:, :], ALU.add).then_inc(elim, 1)
                    pool.tensor_scalar(factor[:, :], column[:, :], inv[:, :], neg[:, :], ALU.mult, ALU.mult).then_inc(elim, 1)
                    pool.wait_ge(elim, base + 10)
                    alone(pool)
                    pool.tensor_scalar(rows, prow[:, 0:RANK], factor[:, :], None, ALU.mult).then_inc(elim, 1)
                    pool.wait_ge(elim, base + 11)
                    pool.tensor_tensor(lu[:, :], lu[:, :], rows, ALU.add).then_inc(elim, 1)

                def batch(b, phase):
                    pool.wait_ge(mv_done, TT * (b + 1))
                    alone(pool)
                    pool.tensor_scalar(rstd[:, 0, :], mv[:, :, 1], LN_EPS, None, ALU.add).then_inc(rstd_step, 1)
                    pool.wait_ge(rstd_step, 2 * b + 1)
                    pool.tensor_tensor(rstd[:, 1, :], rstd[:, 0, :], mhalf[:, :], ALU.pow).then_inc(rstd_step, 1)
                    pool.wait_ge(rstd_step, 2 * b + 2)
                    alone(pool)
                    for tt in range(TT):
                        pool.tensor_scalar(xln[:, tt, :], xln[:, tt, :], mv[:, tt, 0:1], rstd[:, 1, tt:tt + 1],
                                           ALU.subtract, ALU.mult).then_inc(ln_norm, 1)
                    for f in range(KT + 1):
                        rows = PAR if f < KT else REM
                        pool.wait_ge(hT_hi, (KT + 2) * b + (f + 1 if f < KT else KT + 2))
                        part = hT[0:rows, KT + f if f < KT else A_PARTS - 1, :]
                        hi = hT[0:rows, f if f < KT else 2 * KT, :]
                        pool.tensor_tensor(part, hf[f % 2][0:rows, :], f32(hi), ALU.subtract).then_inc(hT_split, 1)
                    pool.wait_ge(gate_in, 16 * (b + 1))
                    pool.tensor_tensor(gb[:, :], gate[:, :], beff[:, :], ALU.mult).then_inc(gb_done, 1)
                    pool.wait_ge(gb_done, b + 1)
                    for h in range(HEADS):
                        pool.wait_ge(o_read, b * HEADS + h + 2)
                        head = oo[:, :, h * HD:(h + 1) * HD]
                        pool.tensor_tensor(head, head, recip[h % 2][:, :].unsqueeze(2).to_broadcast([PAR, TT, HD]), ALU.mult).then_inc(o_norm, 1)
                        (sign_step if phase else cholesky_step)((b - phase * (BATCH // 2)) * HEADS + h)
                    for qt in range(TT):
                        pool.wait_ge(xr_in[qt % 2], 16 * (b * (TT // 2) + qt // 2 + 1))
                        pool.tensor_tensor(xr[qt % 2][:, :], xr[qt % 2][:, :], gb[:, :], ALU.add).then_inc(xr_done, 1)
                        pool.wait_ge(xr_done, b * TT + qt + 1)
                        pool.wait_ge(g_free, b * G_ALL + G_P + 4 * qt + 6)
                        pool.tensor_tensor(xo[qt % 2][:, :], xo[qt % 2][:, :], xr[qt % 2][:, :], ALU.add).then_inc(xo_done, 1)

                for phase in range(2):
                    with pool.Fori(0, BATCH // 2) as i:
                        batch(i + phase * (BATCH // 2), phase)
                    if phase == 0:
                        turn_to_signs()

            @block.scalar
            def _(act):
                act.sem_inc(exp_hi, 2)
                act.sem_inc(ot_done, 1)

                def batch(b):
                    def hT_his(f):
                        act.wait_ge(g_free, b * G_ALL + G_LN + f + 3)
                        if f < KT:
                            act.activation(hT[:, f, :], hf[f % 2][:, :], ACT.Copy).then_inc(hT_hi, 1)
                        else:
                            act.activation(hT[0:REM, 2 * KT, :], hf[f % 2][0:REM, :], ACT.Copy).then_inc(hT_hi, 1)
                            act.activation(hT[REM:PAR, 2 * KT, :], hf[f % 2][0:REM, :], ACT.Copy).then_inc(hT_hi, 1)

                    def v_his(half, tt):
                        g = G_V + TT * half + tt
                        act.wait_ge(g_full, b * G_ALL + g + 1)
                        act.activation(vv[:, tt, 8 * half:8 * half + 8, 0:HD], G[g % 2][:, 0:HALF].rearrange("p (h d) -> p h d", d=HD), ACT.Copy).then_inc(v_hi, 1)

                    def qk_his(t):
                        g = G_QK + t
                        act.wait_ge(g_full, b * G_ALL + g + 1)
                        for (slot, parity), total in MOVES.items():
                            if parity == t % 2 and total:
                                before = MOVES_AFTER[t - 2][slot, parity] if t >= 2 else 0
                                act.wait_ge(moved[slot, parity], 16 * (b * total + before + 1))
                        act.activation(qkhi[t % 2][:, :], G[g % 2][:, :], ACT.Identity, bias=bqk[:, t:t + 1]).then_inc(qk_hi, 1)

                    def copy_mrow(h):
                        act.wait_ge(mT, b * HEADS + h + 1)
                        act.wait_ge(mrow_in[h % 2], 16 * (b * (HEADS // 2) + h // 2 + 1))
                        act.activation(mrow[h % 2][:, :], X[0:TT, 0:PAR], ACT.Copy).then_inc(mrow_done, 1)

                    def probabilities(h, kt):
                        n = (b * HEADS + h) * TT + kt
                        if kt < TT - 1:
                            act.wait_ge(s_full, (b * HEADS + h) * (TT - 1) + kt + 1)
                        else:
                            act.wait_ge(scored, b * HEADS + h + RING + 1)
                        act.wait_ge(p_lo, n + 1)
                        act.activation(pf[kt % 2][:, :], S[kt % 2][:, :], ACT.Exp, scale=SCALE).then_inc(exp_f, 1)
                        act.wait_ge(pv, n + 1)
                        act.activation(phi[kt % 2][:, :], S[kt % 2][:, :], ACT.Exp, scale=SCALE).then_inc(exp_hi, 1)

                    def take_o(h):
                        act.wait_ge(pv, (b * HEADS + h) * TT + TT + 2)
                        act.wait_ge(oT, b * HEADS + h + 1)
                        act.activation(ots[h % 2][:, :], O[0:2 * HD + 1, :], ACT.Copy).then_inc(ot_done, 1)

                    def a_his(qt):
                        g = G_P + 4 * qt
                        act.wait_ge(g_full, b * G_ALL + g + 1)
                        act.activation(aT[:, 0:KT, :], G[g % 2][:, :].rearrange("p (f t) -> p f t", t=PAR), ACT.Copy).then_inc(a_hi, 1)
                        act.wait_ge(g_full, b * G_ALL + g + 2)
                        act.activation(aT[0:REM, 2 * KT, :], G[(g + 1) % 2][0:REM, 0:PAR], ACT.Copy).then_inc(a_hi, 1)
                        act.activation(aT[REM:PAR, 2 * KT, :], G[(g + 1) % 2][0:REM, 0:PAR], ACT.Copy).then_inc(a_hi, 1)

                    for f in range(KT + 1):
                        hT_his(f)
                    for half in range(2):
                        for tt in range(TT):
                            v_his(half, tt)
                    for h in range(HEADS):
                        for t in q_tiles_before(h):
                            qk_his(t)
                        if h == 0:
                            copy_mrow(0)
                        for kt in range(TT):
                            probabilities(h, kt)
                        if h + 1 < HEADS:
                            copy_mrow(h + 1)
                        take_o(h)
                    for qt in range(TT):
                        a_his(qt)

                for phase in range(2):
                    with act.Fori(0, BATCH // 2) as i:
                        batch(i + phase * (BATCH // 2))

            @block.vector
            def _(dve):
                for slot in range(RING):
                    dve.memset(f32(ks[slot][:, :]), 1.0).then_inc(fixed, 1)
                dve.memset(f32(vv[:, :, :, :]), 1.0).then_inc(fixed, 1)
                dve.sem_inc(g_free, 2)
                dve.sem_inc(m_read, 2)
                dve.sem_inc(p_lo, 2)
                dve.sem_inc(o_read, 1)

                def batch(b):
                    def statistics(tt):
                        for half in range(2):
                            dve.bn_stats(stats[:, tt, half, :], xln[:, tt, half * HALF:(half + 1) * HALF]).then_inc(st_done, 1)
                        dve.wait_ge(st_done, (b * TT + tt + 1) * 2)
                        alone(dve)
                        dve.bn_aggr(mv[:, tt, :], stats[:, tt, :, :]).then_inc(mv_done, 1)

                    def modulate(f):
                        rows = PAR if f < KT else REM
                        g = G_LN + f
                        dve.wait_ge(g_full, b * G_ALL + g + 1)
                        dve.wait_ge(hT_split, b * (KT + 1) + f + (1 if f else 2))
                        dve.tensor_scalar(hf[f % 2][0:rows, :], G[g % 2][0:rows, :], adaT[0:rows, 1, f, bass.ds(b, 1)],
                                          adaT[0:rows, 0, f, bass.ds(b, 1)], ALU.mult, ALU.add).then_inc(g_free, 1)

                    def v_los(half, tt):
                        g = G_V + TT * half + tt
                        dve.wait_ge(v_hi, b * 2 * TT + TT * half + tt + 1)
                        heads = vv[:, tt, 8 * half:8 * half + 8, :]
                        dve.tensor_tensor(heads[:, :, HD + 1:2 * HD + 1], G[g % 2][:, 0:HALF].rearrange("p (h d) -> p h d", d=HD),
                                          f32(heads[:, :, 0:HD]), ALU.subtract).then_inc(g_free, 1)

                    def qk_los(t):
                        g = G_QK + t
                        dve.wait_ge(qk_hi, b * QK_TILES + t + 1)
                        dve.scalar_tensor_tensor(qklo[t % 2][:, :], G[g % 2][:, :], bqk[:, t:t + 1], f32(qkhi[t % 2][:, :]),
                                                 ALU.add, ALU.subtract).then_inc(g_free, 1)

                    def row_max(h, qt):
                        n = (b * HEADS + h) * TT + qt
                        dve.wait_ge(m_full, n + 1)
                        dve.tensor_reduce(negm[h % 2][:, qt:qt + 1], M[qt % 2][:, :], AX.X, ALU.max, negate=True).then_inc(m_read, 1)

                    def p_los(h, kt):
                        n = (b * HEADS + h) * TT + kt
                        dve.wait_ge(exp_f, n + 1)
                        dve.wait_ge(exp_hi, n + 3)
                        dve.tensor_tensor(plo[kt % 2][:, :], pf[kt % 2][:, :], f32(phi[kt % 2][:, :]), ALU.subtract).then_inc(p_lo, 1)

                    def read_o(h):
                        dve.wait_ge(oT, b * HEADS + h + 3)
                        if h == 0:
                            dve.wait_ge(g_full, b * G_ALL + G_V)
                        view = X[:, 0:TT * OW].rearrange("p (t c) -> p t c", c=OW)
                        dve.wait_ge(o_norm, b * HEADS + h + 1)
                        dve.reciprocal(recip[h % 2][:, :], view[:, :, HD]).then_inc(recip_done, 1)
                        pair = view[:, :, 0:2 * (HD + 1)].rearrange("p t (two d) -> p t d two", two=2)[:, :, 0:HD, :]
                        dve.wait_ge(recip_done, b * HEADS + h + 1)
                        dve.tensor_reduce(oo[:, :, h * HD:(h + 1) * HD], pair, AX.X, ALU.add).then_inc(o_read, 1)

                    def a_los(qt):
                        g = G_P + 4 * qt
                        dve.wait_ge(a_hi, 3 * (b * TT + qt) + 1)
                        dve.tensor_tensor(aT[:, KT:2 * KT, :], G[g % 2][:, :].rearrange("p (f t) -> p f t", t=PAR),
                                          f32(aT[:, 0:KT, :]), ALU.subtract).then_inc(g_free, 1)
                        dve.wait_ge(a_hi, 3 * (b * TT + qt) + 3)
                        dve.tensor_tensor(aT[0:REM, A_PARTS - 1, :], G[(g + 1) % 2][0:REM, 0:PAR], f32(aT[0:REM, 2 * KT, :]),
                                          ALU.subtract).then_inc(g_free, 1)

                    def gated(qt):
                        dve.wait_ge(x1_out[qt % 2], 16 * (b * (TT // 2) + qt // 2 + 1))
                        if qt == 0:
                            dve.wait_ge(gate_in, 16 * (b + 1))
                        for half in range(2):
                            g = G_P + 4 * qt + 2 + half
                            cols = slice(half * HALF, (half + 1) * HALF)
                            dve.wait_ge(g_full, b * G_ALL + g + 1)
                            dve.tensor_tensor(xo[qt % 2][:, cols], G[g % 2][:, 0:HALF], gate[:, cols], ALU.mult).then_inc(g_free, 1)

                    dve.wait_ge(x_in, 16 * (b + 1))
                    for tt in range(TT):
                        statistics(tt)
                    for f in range(KT + 1):
                        modulate(f)
                    for half in range(2):
                        for tt in range(TT):
                            v_los(half, tt)
                    for h in range(HEADS):
                        for t in q_tiles_before(h):
                            qk_los(t)
                        if h == 0:
                            for qt in range(TT):
                                row_max(0, qt)
                        for kt in range(TT):
                            p_los(h, kt)
                            if h + 1 < HEADS:
                                row_max(h + 1, kt)
                        read_o(h)
                    for qt in range(TT):
                        a_los(qt)
                        gated(qt)

                for phase in range(2):
                    with dve.Fori(0, BATCH // 2) as i:
                        batch(i + phase * (BATCH // 2))

            @block.tensor
            def _(pe):
                pe.sem_inc(scored, RING)
                pe.sem_inc(pv, 2)
                pe.sem_inc(oT, 2)
                pe.wait_ge(fixed, RING + 3)

                def batch(b):
                    def transpose_x(f):
                        rows = PAR if f < KT else REM
                        g = G_LN + f
                        pe.wait_ge(g_free, b * G_ALL + g + 1)
                        alone(pe)
                        for tt in range(TT):
                            if f == 0:
                                pe.wait_ge(ln_norm, b * TT + tt + 1)
                            mm = pe.transpose(G[g % 2][0:rows, tt * PAR:(tt + 1) * PAR], xln[:, tt, f * PAR:f * PAR + rows], ident[:, :])
                        mm.then_inc(g_full, 1)

                    def v_tile(half, tt):
                        g = G_V + TT * half + tt
                        pe.wait_ge(g_free, b * G_ALL + g + 1)
                        for j, (w, a, rows) in enumerate(PASSES):
                            mm = pe.matmul(G[g % 2][:, 0:HALF], hT[0:rows, a, tt * PAR:(tt + 1) * PAR],
                                           wv[0:rows, w, half * HALF:(half + 1) * HALF], start=(j == 0), stop=(j == len(PASSES) - 1))
                        mm.then_inc(g_full, 1)

                    def qk_tile(t):
                        g = G_QK + t
                        pe.wait_ge(g_free, b * G_ALL + g + 1)
                        for j, (w, a, rows) in enumerate(PASSES):
                            mm = pe.matmul(G[g % 2][:, :], wqk[0:rows, w, t * PAR:(t + 1) * PAR], hT[0:rows, a, :],
                                           start=(j == 0), stop=(j == len(PASSES) - 1))
                        mm.then_inc(g_full, 1)

                    def stacked(h):
                        for (slot, parity), total in MOVES.items():
                            n = MOVES_AFTER[last_tile(h)][slot, parity]
                            if slot == h % RING and n:
                                pe.wait_ge(moved[slot, parity], 16 * (b * total + n + 1))

                    def scores_for_max(h, qt):
                        if qt == 0:
                            stacked(h)
                        pe.wait_ge(m_read, (b * HEADS + h) * TT + qt + 1)
                        slot = h % RING
                        pe.matmul(M[qt % 2][:, :], qs[slot][0:STACK, qt * PAR:(qt + 1) * PAR], ks[slot][0:STACK, :],
                                  start=True, stop=True).then_inc(m_full, 1)

                    def transpose_max(h):
                        pe.wait_ge(m_read, (b * HEADS + h) * TT + TT + 2)
                        pe.wait_ge(o_read, b * HEADS + max(h - 1, 0) + 1)
                        pe.transpose(X[0:TT, 0:PAR], negm[h % 2][:, :], ident[:, :]).then_inc(mT, 1)

                    def scores(h, kt):
                        n = (b * HEADS + h) * TT + kt
                        if kt == 0:
                            pe.wait_ge(mrow_in[h % 2], 16 * (b * (HEADS // 2) + h // 2 + 2))
                        pe.wait_ge(exp_hi, n + 1)
                        slot = h % RING
                        pe.matmul(S[kt % 2][:, :], ks[slot][:, kt * PAR:(kt + 1) * PAR], qs[slot][:, :],
                                  start=True, stop=True).then_inc(s_full if kt < TT - 1 else scored, 1)

                    def values(h, kt):
                        n = (b * HEADS + h) * TT + kt
                        if kt == 0:
                            pe.wait_ge(ot_done, b * HEADS + h + 1)
                            if h % 8 == 0:
                                pe.wait_ge(g_free, b * G_ALL + G_V + TT * (h // 8 + 1) + 2)
                        pe.wait_ge(p_lo, n + 3)
                        v = vv[:, kt, h, 0:2 * HD + 1]
                        pe.matmul(O[0:2 * HD + 1, :], v, phi[kt % 2][:, :], start=(kt == 0), stop=False)
                        pe.matmul(O[0:2 * HD + 1, :], v, plo[kt % 2][:, :], start=False, stop=(kt == TT - 1)).then_inc(pv, 1)

                    def transpose_o(h):
                        pe.wait_ge(ot_done, b * HEADS + h + 2)
                        pe.wait_ge(mrow_done, b * HEADS + min(h + 2, HEADS))
                        pe.wait_ge(o_read, b * HEADS + h + 1)
                        for qt in range(TT):
                            mm = pe.transpose(X[:, qt * OW:qt * OW + 2 * HD + 1], ots[h % 2][:, qt * PAR:(qt + 1) * PAR],
                                              ident[0:2 * HD + 1, 0:2 * HD + 1])
                        mm.then_inc(oT, 1)

                    def project(qt):
                        g = G_P + 4 * qt
                        pe.wait_ge(o_norm, (b + 1) * HEADS + 2)
                        pe.wait_ge(g_free, b * G_ALL + g + 1)
                        for f in range(KT):
                            mm = pe.transpose(G[g % 2][:, f * PAR:(f + 1) * PAR], oo[:, qt, f * PAR:(f + 1) * PAR], ident[:, :])
                        mm.then_inc(g_full, 1)
                        pe.wait_ge(g_free, b * G_ALL + g + 2)
                        alone(pe)
                        pe.transpose(G[(g + 1) % 2][0:REM, 0:PAR], oo[:, qt, KT * PAR:C], ident[:, :]).then_inc(g_full, 1)
                        for half in range(2):
                            pe.wait_ge(g_free, b * G_ALL + g + 3 + half)
                            if half == 0:
                                pe.wait_ge(g_free, b * G_ALL + g + 4)
                            for j, (w, a, rows) in enumerate(PASSES):
                                mm = pe.matmul(G[(g + half) % 2][:, 0:HALF], aT[0:rows, a, :], wp[0:rows, w, half * HALF:(half + 1) * HALF],
                                               start=(j == 0), stop=(j == len(PASSES) - 1))
                            mm.then_inc(g_full, 1)

                    for f in range(KT + 1):
                        transpose_x(f)
                    pe.wait_ge(hT_split, (b + 1) * (KT + 1) + 2)
                    for half in range(2):
                        for tt in range(TT):
                            v_tile(half, tt)
                    for h in range(HEADS):
                        for t in q_tiles_before(h):
                            qk_tile(t)
                        if h == 0:
                            for qt in range(TT):
                                scores_for_max(0, qt)
                            transpose_max(0)
                        scores(h, 0)
                        scores(h, 1)
                        for kt in range(TT):
                            if h + 1 < HEADS:
                                scores_for_max(h + 1, kt)
                            values(h, kt)
                            if kt + 2 < TT:
                                scores(h, kt + 2)
                        if h + 1 < HEADS:
                            transpose_max(h + 1)
                        transpose_o(h)
                    for qt in range(TT):
                        project(qt)

                for phase in range(2):
                    with pe.Fori(0, BATCH // 2) as i:
                        batch(i + phase * (BATCH // 2))
        acts.close()
        attn.close()

        FT = FF // PAR
        w1 = sb(every, "w1", [PAR, W_PARTS, FF], fp32r)
        w2 = sb(every, "w2", [PAR, FT, 2, C], fp32r)
        b1 = sb(every, "b1", [PAR, FT])
        UT = sb(every, "UT", [RANK, C])
        rot = ExitStack()
        VC = 128
        NV = RANK * RANK // VC
        wr = [sb(rot, f"wr{i}", [PAR, KT + 1, VC]) for i in range(2)]
        brc = [sb(rot, f"brc{i}", [BATCH, VC]) for i in range(2)]
        vrow = [sb(rot, f"vrow{i}", [BATCH, VC]) for i in range(2)]
        wst = [sb(rot, f"wst{i}", [PAR, C]) for i in range(3)]
        SQ = [RANK, BATCH, RANK]
        skew, nskew, y1, y2, y3 = (sb(rot, n, SQ) for n in ("skew", "nskew", "y1", "y2", "y3"))
        ev, od, R, RT = (sb(rot, n, SQ) for n in ("ev", "od", "R", "RT"))
        over = sb(rot, "over", [RANK, SQUARINGS, BATCH])
        take = sb(rot, "take", [RANK, BATCH])
        half_of = sb(rot, "half_of", [RANK, SQUARINGS, BATCH])
        sq_sum = sb(rot, "sq_sum", [RANK, BATCH])
        frob = sb(rot, "frob", [RANK, BATCH])
        ones64 = sb(rot, "ones64", [RANK, RANK])
        upper = sb(rot, "upper", [RANK, RANK])
        linvT = sb(rot, "linvT", [RANK, RANK])
        su = sb(rot, "su", [RANK, 1])
        prows = sb(rot, "prows", [RANK, C])
        esb = [sb(rot, f"esb{i}", [PAR, BATCH, RANK]) for i in range(2)]
        eye8 = prows[:, 0:BATCH * RANK].rearrange("p (b j) -> p b j", j=RANK)

        wr_in, brc_in = [sem("wr_in0"), sem("wr_in1")], [sem("brc_in0"), sem("brc_in1")]
        vmm, vrow_done, vrow_out = sem("vmm"), sem("vrow_done"), [sem("vrow_out0"), sem("vrow_out1")]
        skew_in, prows_in, ones_set = sem("skew_in"), sem("prows_in"), sem("ones_set")
        rmm, rstep, sq_mm, sq_done = sem("rmm"), sem("rstep"), sem("sq_mm"), sem("sq_done")
        linv_mm, linv_done, ut_mm, ut_done = sem("linv_mm"), sem("linv_done"), sem("ut_mm"), sem("ut_done")
        e_mm, e_done, e_out = sem("e_mm"), sem("e_done"), [sem("e_out0"), sem("e_out1")]
        wst_in, whi, wlo = [sem(f"wst_in{i}") for i in range(3)], sem("whi"), sem("wlo")
        b1_in, rmm_in, over_set, take_set = sem("b1_in"), sem("rmm_in"), sem("over_set"), sem("take_set")

        WS = []
        for q in range(FF // C):
            cols = slice(q * C, (q + 1) * C)
            for t in range(KT + 1):
                if t < KT:
                    WS.append((w_fc1[t * PAR:(t + 1) * PAR, cols], w1[:, t, cols], w1[:, KT + t, cols], PAR))
                else:
                    WS.append((w_fc1[KT * PAR:C, cols], w1[0:REM, 2 * KT, cols], w1[REM:PAR, 2 * KT, cols], REM))
        for t in range(FT):
            WS.append((w_fc2[t * PAR:(t + 1) * PAR, :], w2[:, t, 0, :], w2[:, t, 1, :], PAR))

        def flat(m):
            return m[:, :, :].rearrange("p b j -> p (b j)")

        with nc.Block() as block:
            @block.sync
            def _(sp):
                sp.dma_start(prows[:, :], p_rows).then_inc(prows_in, 16)
                sp.dma_start(b1[:, :], b_fc1).then_inc(b1_in, 16)
                for v in range(NV):
                    cols = slice(v * VC, (v + 1) * VC)
                    if v >= 2:
                        sp.wait_ge(vmm, v - 1)
                        sp.wait_ge(vrow_done, v - 1)
                    sp.dma_start(wr[v % 2][:, 0:KT, :], w_rot[0:KT * PAR, cols].rearrange("(k p) n -> p k n", p=PAR)).then_inc(wr_in[v % 2], 16)
                    sp.dma_start(wr[v % 2][0:REM, KT, :], w_rot[KT * PAR:C, cols]).then_inc(wr_in[v % 2], 16)
                    sp.dma_start(brc[v % 2][:, :], b_rot[:, cols].partition_broadcast(BATCH)).then_inc(brc_in[v % 2], 16)
                    if v >= 1:
                        sp.wait_ge(vrow_done, v)
                        sp.dma_start(rot_d[:, (v - 1) * VC:v * VC], vrow[(v - 1) % 2][:, :]).then_inc(vrow_out[(v - 1) % 2], 16)
                sp.wait_ge(vrow_done, NV)
                sp.dma_start(rot_d[:, (NV - 1) * VC:NV * VC], vrow[(NV - 1) % 2][:, :]).then_inc(vrow_out[(NV - 1) % 2], 16)
                for p in range(2):
                    sp.wait_ge(vrow_out[p], 16 * (NV // 2))
                sp.dma_start(skew[:, :, :], rot_d.rearrange("b (i j) -> i b j", j=RANK)).then_inc(skew_in, 16)
                for n, (src, hi, lo, rows) in enumerate(WS):
                    if n >= 3:
                        sp.wait_ge(wlo, n - 2)
                    sp.dma_start(wst[n % 3][0:rows, :], src).then_inc(wst_in[n % 3], 16)
                for f in range(KT + 1):
                    rows = PAR if f < KT else REM
                    sp.wait_ge(e_done, f + 1)
                    sp.dma_start(e_d[:, 0:rows, f * RANK:(f + 1) * RANK].rearrange("b p e -> p b e"), esb[f % 2][0:rows, :, :]).then_inc(e_out[f % 2], 16)
                for p in range(2):
                    sp.wait_ge(e_out[p], 16 * (3 - p))
                sp.wait_ge(b1_in, 16)

            @block.gpsimd
            def _(pool):
                for n, (src, hi, lo, rows) in enumerate(WS):
                    pool.wait_ge(whi, n + 1)
                    if n:
                        pool.wait_ge(wlo, n)
                    pool.tensor_tensor(lo, wst[n % 3][0:rows, :], f32(hi), ALU.subtract).then_inc(wlo, 1)

            @block.scalar
            def _(act):
                for n, (src, hi, lo, rows) in enumerate(WS):
                    act.wait_ge(wst_in[n % 3], 16 * (n // 3 + 1))
                    act.activation(hi, wst[n % 3][0:rows, :], ACT.Copy).then_inc(whi, 1)

            @block.vector
            def _(dve):
                done = [0]

                def step(ins):
                    done[0] += 1
                    ins.then_inc(rstep, 1)
                    dve.wait_ge(rstep, done[0])

                step(dve.memset(ones64[:, :], 1.0))
                step(dve.tensor_scalar(upper[:, :], below[:, :], 2.0, 1.0, ALU.mult, ALU.add))
                step(dve.tensor_tensor(su[:, :], scol[:, :], invroot[:, :], ALU.mult))
                dve.wait_ge(linv_mm, 1)
                dve.tensor_copy(linvT[:, :], PB[2][0:RANK, 0:RANK]).then_inc(linv_done, 1)
                dve.wait_ge(ut_mm, 1)
                for half in range(2):
                    dve.tensor_scalar(UT[:, half * HALF:(half + 1) * HALF], PB[3 + half][0:RANK, 0:HALF], su[:, 0:1], None, ALU.mult).then_inc(ut_done, 1)
                for v in range(NV):
                    dve.wait_ge(vmm, v + 1)
                    dve.wait_ge(brc_in[v % 2], 16 * (v // 2 + 1))
                    if v >= 2:
                        dve.wait_ge(vrow_out[v % 2], 16 * (v // 2))
                    dve.tensor_tensor(vrow[v % 2][:, :], PB[v % 2][0:BATCH, 0:VC], brc[v % 2][:, :], ALU.add).then_inc(vrow_done, 1)
                dve.wait_ge(skew_in, 16)
                step(dve.tensor_tensor(skew[:, :, :], skew[:, :, :], upper[:, :].unsqueeze(1).to_broadcast(SQ), ALU.mult))
                step(dve.tensor_tensor(y1[:, :, :], skew[:, :, :], skew[:, :, :], ALU.mult))
                dve.tensor_reduce(sq_sum[:, :], y1[:, :, :], AX.X, ALU.add).then_inc(rmm_in, 1)
                dve.wait_ge(rmm, 1)
                step(dve.tensor_copy(frob[:, :], PB[5][0:RANK, 0:BATCH]))
                for k in range(SQUARINGS):
                    dve.tensor_scalar(over[:, k, :], frob[:, :], 4.0 * 4.0 ** k, None, ALU.is_gt).then_inc(over_set, 1)
                dve.wait_ge(over_set, SQUARINGS)
                step(dve.tensor_scalar(half_of[:, :, :], over[:, :, :], -0.5, 1.0, ALU.mult, ALU.add))
                n = SQUARINGS
                while n > 1:
                    n //= 2
                    step(dve.tensor_tensor(half_of[:, 0:n, :], half_of[:, 0:n, :], half_of[:, n:2 * n, :], ALU.mult))
                step(dve.tensor_tensor(skew[:, :, :], skew[:, :, :], half_of[:, 0, :].unsqueeze(2).to_broadcast(SQ), ALU.mult))
                dve.tensor_scalar(nskew[:, :, :], skew[:, :, :], -1.0, None, ALU.mult).then_inc(rmm_in, 1)
                for n, y in enumerate((y1, y2, y3)):
                    dve.wait_ge(rmm, n + 2)
                    dve.tensor_copy(flat(y), PB[5][0:RANK, :]).then_inc(rmm_in, 1)
                eye = ident[0:RANK, 0:RANK].unsqueeze(1).to_broadcast(SQ)
                c = TAYLOR
                dve.wait_ge(rmm_in, 5)

                def series(out, c0, c1, c2, c3):
                    step(dve.tensor_scalar(flat(out), flat(y1), c1, None, ALU.mult))
                    step(dve.scalar_tensor_tensor(out=flat(out), in0=flat(y2), scalar=c2, in1=flat(out), op0=ALU.mult, op1=ALU.add))
                    if c3:
                        step(dve.scalar_tensor_tensor(out=flat(out), in0=flat(y3), scalar=c3, in1=flat(out), op0=ALU.mult, op1=ALU.add))
                    step(dve.tensor_scalar(flat(RT), diag8(), c0, None, ALU.mult))
                    step(dve.tensor_tensor(flat(out), flat(out), flat(RT), ALU.add))

                def diag8():
                    return flat(eye8)

                step(dve.tensor_copy(eye8[:, :, :], eye))
                series(ev, c[6], c[8], c[10], c[12])
                series(od, c[7], c[9], c[11], 0.0)
                dve.tensor_copy(flat(R), flat(ev)).then_inc(rmm_in, 1)
                dve.wait_ge(rmm, 6)
                series(ev, c[0], c[2], c[4], 0.0)
                step(dve.tensor_tensor(flat(ev), flat(ev), PB[6][0:RANK, :], ALU.add))
                step(dve.tensor_copy(flat(R), flat(od)))
                series(od, c[1], c[3], c[5], 0.0)
                dve.tensor_tensor(flat(od), flat(od), PB[7][0:RANK, :], ALU.add).then_inc(rmm_in, 1)
                dve.wait_ge(rmm, 7)
                dve.tensor_tensor(flat(R), flat(ev), PB[5][0:RANK, :], ALU.add).then_inc(sq_done, 1)
                dve.tensor_tensor(flat(RT), flat(ev), PB[5][0:RANK, :], ALU.subtract).then_inc(sq_done, 1)
                with dve.Fori(0, SQUARINGS) as k:
                    dve.wait_ge(sq_done, 2 * k + 2)
                    dve.tensor_copy(take[:, :], over[:, bass.ds(k, 1), :].rearrange("p o b -> p (o b)")).then_inc(take_set, 1)
                    took = take[:, :].unsqueeze(2).to_broadcast(SQ).bitcast(mybir.dt.uint32)
                    dve.wait_ge(take_set, k + 1)
                    dve.wait_ge(sq_mm, 2 * k + 2)
                    alone(dve)
                    dve.copy_predicated(R[:, :, :], took, PB[0][0:RANK, :].rearrange("p (b j) -> p b j", j=RANK)).then_inc(sq_done, 1)
                    dve.copy_predicated(RT[:, :, :], took, PB[1][0:RANK, :].rearrange("p (b j) -> p b j", j=RANK)).then_inc(sq_done, 1)
                dve.wait_ge(sq_done, 2 * SQUARINGS + 2)
                dve.tensor_tensor(flat(R), flat(R), flat(eye8), ALU.subtract).then_inc(sq_done, 1)
                for f in range(KT + 1):
                    rows = PAR if f < KT else REM
                    dve.wait_ge(e_mm, f + 1)
                    if f >= 2:
                        dve.wait_ge(e_out[f % 2], 16 * (f // 2))
                    dve.tensor_copy(flat(esb[f % 2])[0:rows, :], PB[2 + f % 2][0:rows, :]).then_inc(e_done, 1)

            @block.tensor
            def _(pe):
                pe.transpose(PB[2][0:RANK, 0:RANK], chol[:, RANK:2 * RANK], ident[0:RANK, 0:RANK]).then_inc(linv_mm, 1)
                pe.wait_ge(linv_done, 1)
                pe.wait_ge(prows_in, 16)
                for half in range(2):
                    mm = pe.matmul(PB[3 + half][0:RANK, 0:HALF], linvT[:, :], prows[:, half * HALF:(half + 1) * HALF], start=True, stop=True)
                mm.then_inc(ut_mm, 1)
                for v in range(NV):
                    pe.wait_ge(wr_in[v % 2], 32 * (v // 2 + 1))
                    if v >= 2:
                        pe.wait_ge(vrow_done, v - 1)
                    for t in range(KT + 1):
                        rows = PAR if t < KT else REM
                        mm = pe.matmul(PB[v % 2][0:BATCH, 0:VC], siluT[0:rows, t, :], wr[v % 2][0:rows, t, :], start=(t == 0), stop=(t == KT))
                    mm.then_inc(vmm, 1)

                def products(bank, left, right, done):
                    for b in range(BATCH):
                        mm = pe.matmul(bank[0:RANK, b * RANK:(b + 1) * RANK], left[:, b, :], right[:, b, :], start=True, stop=True)
                    if done is not None:
                        mm.then_inc(done, 1)

                pe.wait_ge(rmm_in, 1)
                pe.matmul(PB[5][0:RANK, 0:BATCH], ones64[:, :], sq_sum[:, :], start=True, stop=True).then_inc(rmm, 1)
                pe.wait_ge(rmm_in, 2)
                products(PB[5], nskew, skew, rmm)
                pe.wait_ge(rmm_in, 3)
                products(PB[5], y1, y1, rmm)
                pe.wait_ge(rmm_in, 4)
                products(PB[5], y1, y2, rmm)
                pe.wait_ge(rmm_in, 6)
                products(PB[6], y3, R, rmm)
                products(PB[7], y3, od, rmm)
                pe.wait_ge(rmm_in, 7)
                products(PB[5], nskew, od, rmm)
                with pe.Fori(0, SQUARINGS) as k:
                    pe.wait_ge(sq_done, 2 * k + 2)
                    alone(pe)
                    products(PB[0], RT, R, sq_mm)
                    products(PB[1], R, RT, sq_mm)
                pe.wait_ge(sq_done, 2 * SQUARINGS + 3)
                pe.wait_ge(ut_done, 2)
                for f in range(KT + 1):
                    rows = PAR if f < KT else REM
                    if f >= 2:
                        pe.wait_ge(e_done, f - 1)
                    pe.matmul(PB[2 + f % 2][0:rows, :], UT[:, f * PAR:f * PAR + rows], flat(R), start=True, stop=True).then_inc(e_mm, 1)
        rot.close()

        CH = 2 * PAR
        CT, NC = CH // PAR, TOKENS // CH
        mlp = ExitStack()
        every.enter_context(mlp)
        xa = sb(mlp, "xa", [PAR, CT, C])
        xs = sb(mlp, "xs", [PAR, CT, C])
        stats2 = sb(mlp, "stats2", [PAR, CT, 2, 6])
        mv2 = sb(mlp, "mv2", [PAR, CT, 2])
        rstd2 = sb(mlp, "rstd2", [PAR, 2, CT])
        mhalf2 = sb(mlp, "mhalf2", [PAR, CT])
        hg = [sb(mlp, f"hg{i}", [PAR, CH]) for i in range(2)]
        h2T = sb(mlp, "h2T", [PAR, A_PARTS, CH], fp32r)
        gf = [sb(mlp, f"gf{i}", [PAR, CH]) for i in range(2)]
        ghi = [sb(mlp, f"ghi{i}", [PAR, CH], fp32r) for i in range(2)]
        glo = [sb(mlp, f"glo{i}", [PAR, CH], fp32r) for i in range(2)]
        x2T = sb(mlp, "x2T", [PAR, KT + 1, CH])
        dzT = sb(mlp, "dzT", [RANK, CH])
        ecur = sb(mlp, "ecur", [PAR, KT + 1, RANK])
        gate2 = sb(mlp, "gate2", [PAR, C])
        gb2 = sb(mlp, "gb2", [PAR, C])
        tmp = sb(mlp, "tmp", [PAR, HALF])

        Y, F, G = PB[0:4], PB[4:6], PB[6:8]
        H_LN, H_X2, H_Z, H_OUT = 0, KT + 1, 2 * (KT + 1), 2 * (KT + 1) + 1
        H_ALL = H_OUT + 2 * CT
        xa_in, xs_in, xs_out = sem("xa_in"), sem("xs_in"), sem("xs_out")
        st2, mv2_done, rstd2_step, ln2, h_hi, h_split = sem("st2"), sem("mv2_done"), sem("rstd2_step"), sem("ln2"), sem("h_hi"), sem("h_split")
        k_full, k_free = sem("k_full"), sem("k_free")
        f_full, gelu_f, gelu_hi, g_lo, fc2_mm, y_full, y_read = (sem(n) for n in ("f_full", "gelu_f", "gelu_hi", "g_lo", "fc2_mm", "y_full", "y_read"))
        gate2_in, e_in, gb2_done, xs_biased, x2_done, x2T_done, dz_done, out_done = (sem(n) for n in ("gate2_in", "e_in", "gb2_done", "xs_biased", "x2_done", "x2T_done", "dz_done", "out_done"))
        fixed2 = sem("fixed2")
        x1c = x1_d.rearrange("b (t p) c -> b p t c", p=PAR)
        outc = out.rearrange("b (t p) c -> b p t c", p=PAR)

        with nc.Block() as block:
            @block.sync
            def _(sp):
                sp.sem_inc(xs_out, 16)
                with sp.Fori(0, BATCH) as b:
                    for j in range(NC):
                        n = b * NC + j
                        span = slice(j * CT, (j + 1) * CT)
                        sp.wait_ge(xs_out, 16 * (n + 1))
                        sp.dma_start(xs[:, :, :].unsqueeze(1), x1c[bass.ds(b, 1), :, span, :].rearrange("o p t c -> p o t c")).then_inc(xs_in, 16)
                        sp.wait_ge(k_free, n * H_ALL + 2)
                        sp.dma_start(xa[:, :, :].unsqueeze(1), x1c[bass.ds(b, 1), :, span, :].rearrange("o p t c -> p o t c")).then_inc(xa_in, 16)
                        if j == 0:
                            sp.dma_start(gate2[:, :], ada_d[bass.ds(b, 1), 5 * C:6 * C].partition_broadcast(PAR)).then_inc(gate2_in, 16)
                            sp.wait_ge(gb2_done, 2 * b + 1)
                            sp.dma_start(gb2[:, :], b_fc2.partition_broadcast(PAR)).then_inc(gate2_in, 16)
                            sp.dma_start(ecur[:, 0:KT, :].unsqueeze(1), e_d[bass.ds(b, 1), :, 0:KT * RANK].rearrange("o p (f e) -> p o f e", e=RANK)).then_inc(e_in, 16)
                            sp.dma_start(ecur[0:REM, KT, :].unsqueeze(1), e_d[bass.ds(b, 1), 0:REM, KT * RANK:(KT + 1) * RANK].rearrange("o p e -> p o e")).then_inc(e_in, 16)
                        sp.wait_ge(out_done, 2 * CT * (n + 1))
                        sp.dma_start(outc[bass.ds(b, 1), :, span, :].rearrange("o p t c -> p o t c"), xs[:, :, :].unsqueeze(1)).then_inc(xs_out, 16)
                sp.wait_ge(xs_out, 16 * (BATCH * NC + 1))

            @block.gpsimd
            def _(pool):
                pool.memset(mhalf2[:, :], -0.5).then_inc(fixed2, 1)
                pool.wait_ge(fixed2, 1)
                pool.sem_inc(h_split, 2)
                pool.sem_inc(gb2_done, 1)
                with pool.Fori(0, BATCH) as b:
                    for j in range(NC):
                        n = b * NC + j
                        pool.wait_ge(mv2_done, CT * (n + 1))
                        alone(pool)
                        pool.tensor_scalar(rstd2[:, 0, :], mv2[:, :, 1], LN_EPS, None, ALU.add).then_inc(rstd2_step, 1)
                        pool.wait_ge(rstd2_step, 2 * n + 1)
                        pool.tensor_tensor(rstd2[:, 1, :], rstd2[:, 0, :], mhalf2[:, :], ALU.pow).then_inc(rstd2_step, 1)
                        pool.wait_ge(rstd2_step, 2 * n + 2)
                        alone(pool)
                        for tt in range(CT):
                            pool.tensor_scalar(xa[:, tt, :], xa[:, tt, :], mv2[:, tt, 0:1], rstd2[:, 1, tt:tt + 1],
                                               ALU.subtract, ALU.mult).then_inc(ln2, 1)
                        for f in range(KT + 1):
                            rows = PAR if f < KT else REM
                            pool.wait_ge(h_hi, (KT + 2) * n + (f + 1 if f < KT else KT + 2))
                            part = h2T[0:rows, KT + f if f < KT else A_PARTS - 1, :]
                            hi = h2T[0:rows, f if f < KT else 2 * KT, :]
                            pool.tensor_tensor(part, hg[(5 * j + f) % 2][0:rows, :], f32(hi), ALU.subtract).then_inc(h_split, 1)
                        if j == 0:
                            pool.wait_ge(gate2_in, 32 * (b + 1))
                            pool.tensor_tensor(gb2[:, :], gate2[:, :], gb2[:, :], ALU.mult).then_inc(gb2_done, 1)
                            pool.wait_ge(gb2_done, 2 * b + 2)
                        pool.wait_ge(xs_in, 16 * (n + 1))
                        for tt in range(CT):
                            last = pool.tensor_tensor(xs[:, tt, :], xs[:, tt, :], gb2[:, :], ALU.add)
                            last.then_inc(xs_biased, 1)
                        if j == NC - 1:
                            pool.wait_ge(xs_biased, CT * (n + 1))
                            pool.sem_inc(gb2_done, 1)

            @block.scalar
            def _(act):
                act.sem_inc(gelu_hi, 2)
                with act.Fori(0, BATCH) as b:
                    for j in range(NC):
                        n = b * NC + j
                        for f in range(KT + 1):
                            src = hg[(5 * j + f) % 2]
                            act.wait_ge(k_free, n * H_ALL + H_LN + f + 3)
                            if f < KT:
                                act.activation(h2T[:, f, :], src[:, :], ACT.Copy).then_inc(h_hi, 1)
                            else:
                                act.activation(h2T[0:REM, 2 * KT, :], src[0:REM, :], ACT.Copy).then_inc(h_hi, 1)
                                act.activation(h2T[REM:PAR, 2 * KT, :], src[0:REM, :], ACT.Copy).then_inc(h_hi, 1)
                        for ft in range(FT):
                            m = n * FT + ft
                            act.wait_ge(f_full, m + 1)
                            act.wait_ge(g_lo, m + 1)
                            act.activation(gf[ft % 2][:, :], F[ft % 2][:, 0:CH], ACT.Gelu_apprx_tanh, bias=b1[:, ft:ft + 1]).then_inc(gelu_f, 1)
                            act.wait_ge(fc2_mm, m + 1)
                            act.activation(ghi[ft % 2][:, :], F[ft % 2][:, 0:CH], ACT.Gelu_apprx_tanh, bias=b1[:, ft:ft + 1]).then_inc(gelu_hi, 1)
                        for f in range(KT + 1):
                            rows = PAR if f < KT else REM
                            g = H_X2 + f
                            act.wait_ge(k_full, n * H_ALL + g + 1)
                            act.activation(x2T[0:rows, f, :], G[(j * H_ALL + g) % 2][0:rows, 0:CH], ACT.Copy).then_inc(x2T_done, 1)
                        act.wait_ge(k_full, n * H_ALL + H_Z + 1)
                        act.activation(dzT[:, :], G[(j * H_ALL + H_Z) % 2][0:RANK, 0:CH], ACT.Copy).then_inc(dz_done, 1)

            @block.vector
            def _(dve):
                dve.sem_inc(g_lo, 2)
                dve.sem_inc(k_free, 2)
                dve.sem_inc(y_read, 1)
                with dve.Fori(0, BATCH) as b:
                    for j in range(NC):
                        n = b * NC + j
                        dve.wait_ge(xa_in, 16 * (n + 1))
                        for tt in range(CT):
                            for half in range(2):
                                dve.bn_stats(stats2[:, tt, half, :], xa[:, tt, half * HALF:(half + 1) * HALF]).then_inc(st2, 1)
                            dve.wait_ge(st2, (n * CT + tt + 1) * 2)
                            alone(dve)
                            dve.bn_aggr(mv2[:, tt, :], stats2[:, tt, :, :]).then_inc(mv2_done, 1)
                        for f in range(KT + 1):
                            rows = PAR if f < KT else REM
                            g = H_LN + f
                            dve.wait_ge(k_full, n * H_ALL + g + 1)
                            dve.wait_ge(h_split, n * (KT + 1) + f + 1)
                            dve.tensor_scalar(hg[(5 * j + f) % 2][0:rows, :], G[(j * H_ALL + g) % 2][0:rows, 0:CH], adaT[0:rows, 3, f, bass.ds(b, 1)],
                                              adaT[0:rows, 2, f, bass.ds(b, 1)], ALU.mult, ALU.add).then_inc(k_free, 1)
                        for ft in range(FT):
                            m = n * FT + ft
                            dve.wait_ge(gelu_f, m + 1)
                            dve.wait_ge(gelu_hi, m + 3)
                            dve.tensor_tensor(glo[ft % 2][:, :], gf[ft % 2][:, :], f32(ghi[ft % 2][:, :]), ALU.subtract).then_inc(g_lo, 1)
                        dve.wait_ge(y_full, n + 1)
                        dve.wait_ge(xs_biased, CT * (n + 1))
                        for tt in range(CT):
                            for half in range(2):
                                m = n * 2 * CT + 2 * tt + half
                                cols = slice(half * HALF, (half + 1) * HALF)
                                dve.tensor_tensor(tmp[:, :], Y[2 * tt + half][:, 0:HALF], gate2[:, cols], ALU.mult).then_inc(y_read, 1)
                                dve.wait_ge(y_read, m + 2)
                                dve.tensor_tensor(xs[:, tt, cols], xs[:, tt, cols], tmp[:, :], ALU.add).then_inc(x2_done, 1)
                                dve.wait_ge(x2_done, m + 1)
                        for f in range(KT + 1):
                            dve.wait_ge(x2T_done, n * (KT + 1) + f + 1)
                            dve.sem_inc(k_free, 1)
                        dve.wait_ge(dz_done, n + 1)
                        dve.sem_inc(k_free, 1)
                        for tt in range(CT):
                            for half in range(2):
                                g = H_OUT + 2 * tt + half
                                cols = slice(half * HALF, (half + 1) * HALF)
                                dve.wait_ge(k_full, n * H_ALL + g + 1)
                                dve.tensor_tensor(xs[:, tt, cols], xs[:, tt, cols], G[(j * H_ALL + g) % 2][:, 0:HALF], ALU.add).then_inc(out_done, 1)
                                dve.wait_ge(out_done, n * 2 * CT + 2 * tt + half + 1)
                                dve.sem_inc(k_free, 1)

            @block.tensor
            def _(pe):
                pe.sem_inc(fc2_mm, 2)
                with pe.Fori(0, BATCH) as b:
                    for j in range(NC):
                        n = b * NC + j

                        def bank(g):
                            pe.wait_ge(k_free, n * H_ALL + g + 1)
                            alone(pe)
                            return G[(j * H_ALL + g) % 2]

                        for f in range(KT + 1):
                            rows = PAR if f < KT else REM
                            to = bank(H_LN + f)
                            for tt in range(CT):
                                if f == 0:
                                    pe.wait_ge(ln2, n * CT + tt + 1)
                                mm = pe.transpose(to[0:rows, tt * PAR:(tt + 1) * PAR], xa[:, tt, f * PAR:f * PAR + rows], ident[:, :])
                            mm.then_inc(k_full, 1)
                        pe.wait_ge(h_split, (n + 1) * (KT + 1) + 2)

                        def fc1(ft):
                            m = n * FT + ft
                            pe.wait_ge(gelu_hi, m + 1)
                            for i, (w, a, rows) in enumerate(PASSES):
                                mm = pe.matmul(F[ft % 2][:, 0:CH], w1[0:rows, w, ft * PAR:(ft + 1) * PAR], h2T[0:rows, a, :],
                                               start=(i == 0), stop=(i == len(PASSES) - 1))
                            mm.then_inc(f_full, 1)

                        def fc2(ft):
                            m = n * FT + ft
                            pe.wait_ge(g_lo, m + 3)
                            for tt in range(CT):
                                span = slice(tt * PAR, (tt + 1) * PAR)
                                for i, (g, w) in enumerate(((ghi, 0), (ghi, 1), (glo, 0))):
                                    for half in range(2):
                                        mm = pe.matmul(Y[2 * tt + half][:, 0:HALF], g[ft % 2][:, span], w2[:, ft, w, half * HALF:(half + 1) * HALF],
                                                       start=(ft == 0 and i == 0), stop=(ft == FT - 1 and i == 2))
                            mm.then_inc(fc2_mm, 1)

                        fc1(0)
                        for ft in range(FT):
                            if ft + 1 < FT:
                                fc1(ft + 1)
                            if ft == 0:
                                pe.wait_ge(y_read, 2 * CT * n + 1)
                            fc2(ft)
                        pe.wait_ge(fc2_mm, (n + 1) * FT + 2)
                        pe.sem_inc(y_full, 1)
                        for f in range(KT + 1):
                            rows = PAR if f < KT else REM
                            to = bank(H_X2 + f)
                            if f == 0:
                                pe.wait_ge(x2_done, 2 * CT * (n + 1))
                            for tt in range(CT):
                                mm = pe.transpose(to[0:rows, tt * PAR:(tt + 1) * PAR], xs[:, tt, f * PAR:f * PAR + rows], ident[:, :])
                            mm.then_inc(k_full, 1)
                        to = bank(H_Z)
                        pe.wait_ge(e_in, 32 * (b + 1))
                        pe.wait_ge(x2T_done, (n + 1) * (KT + 1))
                        for f in range(KT + 1):
                            rows = PAR if f < KT else REM
                            mm = pe.matmul(to[0:RANK, 0:CH], ecur[0:rows, f, :], x2T[0:rows, f, :], start=(f == 0), stop=(f == KT))
                        mm.then_inc(k_full, 1)
                        pe.wait_ge(dz_done, n + 1)
                        for tt in range(CT):
                            for half in range(2):
                                to = bank(H_OUT + 2 * tt + half)
                                pe.matmul(to[:, 0:HALF], dzT[:, tt * PAR:(tt + 1) * PAR], UT[:, half * HALF:(half + 1) * HALF],
                                          start=True, stop=True).then_inc(k_full, 1)


def lay_out(inputs):

    def get(name):
        return np.asarray(inputs[name])

    def tiles(v):
        wide = np.zeros((KT + 1) * PAR, v.dtype)
        wide[:C] = v
        return np.ascontiguousarray(wide.reshape(KT + 1, PAR).T)

    heads = np.arange(C).reshape(HEADS, HD)
    order = np.stack([heads, heads + C], 1).reshape(-1)
    w_qkv, b_qkv = get("L0_cond_W_qkv"), get("L0_cond_b_qkv")
    cond = get("cond_1152")
    cond_t = np.zeros(((KT + 1) * PAR, BATCH), cond.dtype)
    cond_t[:C] = cond.T
    iu, ju = np.triu_indices(RANK, k=1)
    w1, b1 = get("L1_cond_W"), get("L1_cond_b")
    w_rot = np.zeros((C, RANK, RANK), w1.dtype)
    b_rot = np.zeros((RANK, RANK), b1.dtype)
    w_rot[:, iu, ju] = w1.T
    w_rot[:, ju, iu] = w1.T
    b_rot[iu, ju] = b1
    b_rot[ju, iu] = b1
    laid = {
        "x": get("x"), "cond_t": cond_t.reshape(KT + 1, PAR, BATCH),
        "w_ada": get("L0_cond_W_ada"), "b_ada": get("L0_cond_b_ada").reshape(1, -1),
        "w_qk": w_qkv[:, order], "b_qk": b_qkv[order].reshape(QK_TILES, PAR).T,
        "w_v": w_qkv[:, 2 * C:], "b_v": tiles(b_qkv[2 * C:]),
        "w_proj": get("L0_cond_W_proj"), "b_proj": get("L0_cond_b_proj").reshape(1, -1),
        "w_fc1": get("L0_cond_W_fc1"), "b_fc1": get("L0_cond_b_fc1").reshape(FF // PAR, PAR).T,
        "w_fc2": get("L0_cond_W_fc2"), "b_fc2": get("L0_cond_b_fc2").reshape(1, -1),
        "p_cols": get("L1_cond_P"), "p_rows": get("L1_cond_P").T,
        "w_rot": w_rot.reshape(C, RANK * RANK), "b_rot": b_rot.reshape(1, -1),
    }
    return {k: np.ascontiguousarray(v) for k, v in laid.items()}


def declare(nc, laid):
    f = mybir.dt.float32
    aps = {k: nc.dram_tensor(k, v.shape, mybir.dt.from_np(v.dtype), kind="ExternalInput").ap() for k, v in laid.items()}
    for name, shape in (("ada_d", (BATCH, 6 * C)), ("x1_d", (BATCH, TOKENS, C)), ("rot_d", (BATCH, RANK * RANK)),
                        ("e_d", (BATCH, PAR, (KT + 1) * RANK))):
        aps[name] = nc.dram_tensor(name, shape, f).ap()
    aps["out"] = nc.dram_tensor("out", (BATCH, TOKENS, C), f, kind="ExternalOutput").ap()
    build(nc, **aps)


def kernel(**inputs):
    import concourse.bacc as bacc
    from concourse.bass_utils import run_bass_kernel_spmd

    laid = lay_out(inputs)
    nc = bacc.Bacc("TRN2", target_bir_lowering=False, num_devices=1)
    declare(nc, laid)
    r = run_bass_kernel_spmd(nc, [laid], core_ids=[0])
    return r.results[0]["out"]
```

```python
import concourse.bass as bass
import numpy as np
from concourse import mybir
from contextlib import ExitStack

BATCH, TOKENS, C = 8, 512, 576
HEADS = 16
HD = C // HEADS
FF = 4 * C
RANK = 64
PAR = 128
KT = 4
REM = C - KT * PAR
HALF = C // 2
TT = TOKENS // PAR
LN_EPS = 1e-6
SCALE = float(HD) ** -0.5

SQUARINGS = 16
TAYLOR = [1.0]
for _n in range(1, 13):
    TAYLOR.append(TAYLOR[-1] / _n)

W_PARTS, A_PARTS = 2 * KT + 1, 2 * KT + 2
PASSES = []
for _t in range(KT):
    PASSES += [(_t, _t, PAR), (_t, KT + _t, PAR), (KT + _t, _t, PAR)]
PASSES += [(2 * KT, 2 * KT, PAR), (2 * KT, 2 * KT + 1, REM)]

QK_COLS = 2 * C
QK_TILES = QK_COLS // PAR
RING = 4
STACK = 3 * HD
MROW = STACK


def pieces(t):
    out = []
    col = t * PAR
    while col < (t + 1) * PAR:
        block, row = divmod(col, HD)
        n = min(HD - row, (t + 1) * PAR - col)
        out.append((block // 2, block % 2, row, n, col - t * PAR))
        col += n
    return out


MOVES = {(s, p): 0 for s in range(RING) for p in range(2)}
MOVES_AFTER = []
for _t in range(QK_TILES):
    for _h, _k, _r, _n, _p in pieces(_t):
        MOVES[_h % RING, _t % 2] += 3
    MOVES_AFTER.append(dict(MOVES))


def last_tile(h):
    return -(-2 * HD * (h + 1) // PAR) - 1


SLOTS = TT * HEADS
EARLY_QK = 3
FIRST_SLOT = [(0, ("v", 1, 0)), (2, ("v", 1, 1)), (4, ("qk", 3)), (6, ("v", 1, 2)), (7, ("tr", 0)), (9, ("p", 0, 0)),
              (11, ("p", 0, 1)), (11, ("tr", 1)), (12, ("qk", 4)), (14, ("p", 1, 0)), (15, ("p", 1, 1)), (15, ("tr", 2)),
              (16, ("qk", 5)), (18, ("p", 2, 0)), (20, ("p", 2, 1)), (21, ("v", 1, 3)), (23, ("tr", 3)), (24, ("qk", 6)),
              (26, ("p", 3, 0)), (28, ("p", 3, 1)), (32, ("qk", 7)), (36, ("qk", 8)), (43, ("ln", 0)), (44, ("ln", 1)),
              (45, ("ln", 2)), (46, ("ln", 3)), (47, ("ln", 4)), (48, ("v", 0, 0)), (50, ("qk", 0)), (52, ("v", 0, 1)),
              (54, ("qk", 1)), (56, ("v", 0, 2)), (58, ("v", 0, 3)), (60, ("qk", 2))]
IN_ONE_SLOT = [("v", 1, 2), ("p", 0, 1), ("p", 1, 0), ("p", 1, 1), ("p", 2, 1)]
TR_SLOT = [_n for _n, _u in FIRST_SLOT if _u[0] == "tr"]
assert all(_n % TT == TT - 1 for _n in TR_SLOT)
MAX_LEAD = 10
STAT_SLOT, NORM_SLOT, SPLIT_SLOT = 38, 42, 46
LOAD_SLOT, RESIDUAL_SLOT = 35, 49
EARLY = 5
EARLY_SLOT = 28
ACT_LAG, DVE_LAG = 1, 1
ELIM_SLOT = {{10: 43, 11: 47, 12: 50}.get(_h, TT * _h): _h for _h in range(HEADS)}


def shift(unit):
    if unit[0] in ("tr", "p"):
        return -1
    early = {"ln": True, "v": unit[1] == 0, "qk": unit[1] < EARLY_QK}[unit[0]]
    return 1 if early else 0


def is_there(b, n):
    return not isinstance(b, int) or 0 <= b * SLOTS + n < BATCH * SLOTS


PARTS_AT = {n: [] for n in range(SLOTS)}
ENDS_AT = {n: [] for n in range(-2, SLOTS)}
POS, _uses = {}, 0
for _n, _u in FIRST_SLOT:
    _two = _u[0] in ("v", "qk", "p")
    _last = _n + (_two and _u not in IN_ONE_SLOT)
    for _part in range(2 if _two else 1):
        PARTS_AT[min(_n + _part, _last)].append((_u, _part))
    ENDS_AT[_last].append(_u)
    POS[_u] = _uses
    _uses += 1
G_ALL = _uses
G_TABLE, _g = {}, 0
for _it in range(-1, BATCH + 1):
    for _n, _u in FIRST_SLOT:
        if 0 <= _it + shift(_u) < BATCH:
            G_TABLE[_it, _u] = _g
            _g += 1
G_SHIFT = G_TABLE[1, FIRST_SLOT[0][1]] - G_ALL
assert G_ALL % 2 == 0 and G_SHIFT % 2 == 0
for _it in range(0, BATCH):
    for _n, _u in FIRST_SLOT:
        if (_it, _u) in G_TABLE and (_it > 0 or shift(_u) > 0):
            assert G_TABLE[_it, _u] == _it * G_ALL + G_SHIFT + POS[_u]


def g_use(it, unit):
    return G_TABLE[it, unit] if isinstance(it, int) else it * G_ALL + (G_SHIFT + POS[unit])


def g_bank(it, unit):
    return (G_TABLE[it, unit] if isinstance(it, int) else POS[unit]) % 2


def build(nc, x, cond_t, w_ada, b_ada, w_qk, b_qk, w_v, b_v, w_proj, b_proj, w_fc1, b_fc1, w_fc2,
          b_fc2, p_cols, p_rows, w_rot, b_rot, ada_d, x1_d, rot_d, e_d, out):
    fp32, fp32r = mybir.dt.float32, mybir.dt.float32r
    ALU, ACT, AX = mybir.AluOpType, mybir.ActivationFunctionType, mybir.AxisListType
    ADD_ALL = bass.bass_isa.ReduceOp.add
    every = ExitStack()

    def sem(name):
        return every.enter_context(nc.semaphore(name))

    def sb(ctx, name, shape, dt=fp32):
        return ctx.enter_context(nc.sbuf_tensor(name, shape, dt))

    def f32(ap):
        return ap.bitcast(fp32)

    def alone(engine):
        engine.nop(nofuse=True)

    with every:
        PB = [every.enter_context(nc.psum_tensor(f"bank{i}", [PAR, 512], fp32)) for i in range(8)]
        ident = sb(every, "ident", [PAR, PAR])
        adaT = sb(every, "adaT", [PAR, 4, KT + 1, BATCH])
        siluT = sb(every, "siluT", [PAR, KT + 1, BATCH])
        chol = sb(every, "chol", [RANK, 3 * RANK])
        lu = sb(every, "lu", [RANK, RANK])
        dcol = sb(every, "dcol", [RANK, 1])
        scol = sb(every, "scol", [RANK, 1])
        invroot = sb(every, "invroot", [RANK, 1])
        below = sb(every, "below", [RANK, RANK])

        const_ready = sem("const_ready")
        cond_in, bada_in, ada_in0, ada_in1 = sem("cond_in"), sem("bada_in"), sem("ada_in0"), sem("ada_in1")
        ada_in = [ada_in0, ada_in1]
        silu_done, ada_mm, ada_rows, ada_stored = sem("silu_done"), sem("ada_mm"), sem("ada_rows"), sem("ada_stored")
        adaT_mm, adaT_done = sem("adaT_mm"), sem("adaT_done")
        stage_in = [sem(f"stage_in{i}") for i in range(3)]
        hi_done, lo_done, beff_step = sem("hi_done"), sem("lo_done"), sem("beff_step")
        bvec_in, bvb_done, beff_done = sem("bvec_in"), sem("bvb_done"), sem("beff_done")
        p_in, g_mm, chol_init = sem("p_in"), sem("g_mm"), sem("chol_init")

        attn = ExitStack()
        every.enter_context(attn)
        wqk = sb(attn, "wqk", [PAR, W_PARTS, QK_COLS], fp32r)
        wv = sb(attn, "wv", [PAR, W_PARTS, C], fp32r)
        wp = sb(attn, "wp", [PAR, W_PARTS, C], fp32r)
        bias2 = sb(attn, "bias2", [33, C], fp32r)
        bqk = sb(attn, "bqk", [PAR, QK_TILES])
        stages = ExitStack()
        cond = sb(stages, "cond", [PAR, KT + 1, BATCH])
        bada = sb(stages, "bada", [BATCH, 6 * C])
        ada = sb(stages, "ada", [BATCH, 6 * C])
        wada = [sb(stages, f"wada{i}", [PAR, KT + 1, 512]) for i in range(2)]
        stage = [sb(stages, f"stage{i}", [PAR, QK_COLS]) for i in range(3)]
        bv = sb(stages, "bv", [PAR, KT + 1])
        beff = sb(stages, "beff", [PAR, C])
        bhi = sb(stages, "bhi", [PAR, C], fp32r)
        bproj = sb(stages, "bproj", [PAR, C])
        bvb = sb(stages, "bvb", [PAR, KT + 1, PAR])
        pcol = sb(stages, "pcol", [PAR, KT + 1, RANK])
        ptop = sb(stages, "ptop", [RANK, RANK])

        ADA_CHUNKS = [(i, min(512, 6 * C - i)) for i in range(0, 6 * C, 512)]
        SPLITS = [(w_proj, wp, C), (w_qk, wqk, QK_COLS), (w_v, wv, C)]
        STAGES = [(src, dst, n, t) for src, dst, n in SPLITS for t in range(KT + 1)]

        with nc.Block() as block:
            @block.sync
            def _(sp):
                sp.dma_start(cond[:, :, :], cond_t.rearrange("k p b -> p k b")).then_inc(cond_in, 16)
                sp.dma_start(bada[:, :], b_ada.partition_broadcast(BATCH)).then_inc(bada_in, 16)
                sp.dma_start(bv[:, :], b_v).then_inc(bvec_in, 16)
                sp.dma_start(bqk[:, :], b_qk).then_inc(bvec_in, 16)
                sp.dma_start(bproj[:, :], b_proj.partition_broadcast(PAR)).then_inc(bvec_in, 16)
                sp.dma_start(pcol[:, 0:KT, :], p_cols[0:KT * PAR, :].rearrange("(k p) d -> p k d", p=PAR)).then_inc(p_in, 16)
                sp.dma_start(pcol[0:REM, KT, :], p_cols[KT * PAR:C, :]).then_inc(p_in, 16)
                sp.dma_start(ptop[:, :], p_rows[:, 0:RANK]).then_inc(p_in, 16)
                for i, (c0, n) in enumerate(ADA_CHUNKS):
                    if i >= 2:
                        sp.wait_ge(ada_mm, i - 1)
                    sp.dma_start(wada[i % 2][:, 0:KT, 0:n], w_ada[0:KT * PAR, c0:c0 + n].rearrange("(k p) n -> p k n", p=PAR)).then_inc(ada_in[i % 2], 16)
                    sp.dma_start(wada[i % 2][0:REM, KT, 0:n], w_ada[KT * PAR:C, c0:c0 + n]).then_inc(ada_in[i % 2], 16)
                for i, (src, dst, n, t) in enumerate(STAGES):
                    if i >= 3:
                        sp.wait_ge(lo_done, i - 2)
                        if i - 3 <= KT:
                            sp.wait_ge(beff_step, i - 2)
                    rows = PAR if t < KT else REM
                    sp.dma_start(stage[i % 3][0:rows, 0:n], src[t * PAR:t * PAR + rows, :]).then_inc(stage_in[i % 3], 16)
                sp.wait_ge(ada_rows, len(ADA_CHUNKS))
                sp.dma_start(ada_d, ada[:, :]).then_inc(ada_stored, 16)
                sp.wait_ge(ada_stored, 16)

            @block.gpsimd
            def _(pool):
                pool.memset(ident[:, :], 0.0).then_inc(const_ready, 1)
                pool.memset(below[:, :], 0.0).then_inc(const_ready, 1)
                pool.memset(dcol[:, :], 0.0).then_inc(const_ready, 1)
                pool.memset(scol[:, :], 0.0).then_inc(const_ready, 1)
                pool.wait_ge(const_ready, 4)
                pool.affine_select(out=ident[:, :], in_=ident[:, :], compare_op=ALU.not_equal, fill=1.0, base=0,
                                   pattern=[[-1, PAR]], channel_multiplier=1).then_inc(const_ready, 1)
                pool.affine_select(out=below[:, :], in_=below[:, :], compare_op=ALU.is_ge, fill=-1.0, base=0,
                                   pattern=[[1, RANK]], channel_multiplier=-1).then_inc(const_ready, 1)

            @block.scalar
            def _(act):
                act.wait_ge(cond_in, 16)
                act.activation(siluT[:, :, :], cond[:, :, :], ACT.Silu).then_inc(silu_done, 1)
                for i, (src, dst, n, t) in enumerate(STAGES):
                    rows = PAR if t < KT else REM
                    act.wait_ge(stage_in[i % 3], 16 * (i // 3 + 1))
                    act.activation(dst[0:rows, t if t < KT else 2 * KT, :], stage[i % 3][0:rows, 0:n], ACT.Copy).then_inc(hi_done, 1)

            @block.vector
            def _(dve):
                dve.wait_ge(bvec_in, 48)
                dve.memset(bvb[:, :, :], 1.0).then_inc(bvb_done, 1)
                dve.wait_ge(bvb_done, 1)
                for t in range(KT + 1):
                    dve.tensor_scalar(bvb[:, t, :], bvb[:, t, :], bv[:, t:t + 1], None, ALU.mult).then_inc(bvb_done, 1)
                dve.wait_ge(g_mm, 1)
                dve.wait_ge(const_ready, 6)
                dve.tensor_copy(chol[:, 0:RANK], PB[5][0:RANK, 0:RANK]).then_inc(chol_init, 1)
                dve.tensor_copy(chol[:, RANK:2 * RANK], ident[0:RANK, 0:RANK]).then_inc(chol_init, 1)
                dve.tensor_copy(chol[:, 2 * RANK:3 * RANK], ptop[:, :]).then_inc(chol_init, 1)
                dve.wait_ge(bada_in, 16)
                for i, (c0, n) in enumerate(ADA_CHUNKS):
                    dve.wait_ge(ada_mm, i + 1)
                    dve.tensor_tensor(ada[:, c0:c0 + n], PB[i % 2][0:BATCH, 0:n], bada[:, c0:c0 + n], ALU.add).then_inc(ada_rows, 1)
                dve.wait_ge(adaT_mm, 1)
                for j in range(4):
                    for rows, f0, f1 in ((PAR, 0, KT), (REM, KT, KT + 1)):
                        dve.tensor_scalar(adaT[0:rows, j, f0:f1, :],
                                          PB[4][0:rows, 40 * j + 8 * f0:40 * j + 8 * f1].rearrange("p (f b) -> p f b", b=BATCH),
                                          float(j % 2), None, ALU.add).then_inc(adaT_done, 1)
                for i, (src, dst, n, t) in enumerate(STAGES):
                    dve.wait_ge(hi_done, i + 1)
                    if t < KT:
                        dve.tensor_tensor(dst[:, KT + t, :], stage[i % 3][:, 0:n], f32(dst[:, t, :]), ALU.subtract).then_inc(lo_done, 1)
                    else:
                        dve.tensor_tensor(dst[REM:PAR, 2 * KT, :], stage[i % 3][0:REM, 0:n], f32(dst[0:REM, 2 * KT, :]), ALU.subtract).then_inc(lo_done, 1)
                    if i == KT:
                        dve.wait_ge(beff_step, KT + 1)
                        for half in range(2):
                            dve.tensor_tensor(beff[:, half * HALF:(half + 1) * HALF], PB[2 + half][:, 0:HALF],
                                              bproj[:, half * HALF:(half + 1) * HALF], ALU.add).then_inc(beff_done, 1)
                        dve.memset(f32(bias2[:, :]), 0.0).then_inc(beff_done, 1)
                        dve.wait_ge(beff_done, 3)
                        dve.tensor_copy(bhi[:, :], beff[:, :]).then_inc(beff_done, 1)
                        dve.tensor_copy(bias2[0:1, :], beff[0:1, :]).then_inc(beff_done, 1)
                        dve.wait_ge(beff_done, 4)
                        dve.tensor_tensor(bias2[32:33, :], beff[32:33, :], f32(bhi[32:33, :]), ALU.subtract).then_inc(beff_done, 1)

            @block.tensor
            def _(pe):
                pe.wait_ge(p_in, 48)
                for t in range(KT + 1):
                    rows = PAR if t < KT else REM
                    mm = pe.matmul(PB[5][0:RANK, 0:RANK], pcol[0:rows, t, :], pcol[0:rows, t, :], start=(t == 0), stop=(t == KT))
                mm.then_inc(g_mm, 1)
                pe.wait_ge(silu_done, 1)
                for i, (c0, n) in enumerate(ADA_CHUNKS):
                    pe.wait_ge(ada_in[i % 2], 32 * (i // 2 + 1))
                    if i >= 2:
                        pe.wait_ge(ada_rows, i - 1)
                    for t in range(KT + 1):
                        rows = PAR if t < KT else REM
                        mm = pe.matmul(PB[i % 2][0:BATCH, 0:n], siluT[0:rows, t, :], wada[i % 2][0:rows, t, 0:n], start=(t == 0), stop=(t == KT))
                    mm.then_inc(ada_mm, 1)
                pe.wait_ge(ada_rows, len(ADA_CHUNKS))
                pe.wait_ge(const_ready, 6)
                for j, section in enumerate((0, 1, 3, 4)):
                    for f in range(KT + 1):
                        rows, c0 = (PAR if f < KT else REM), section * C + f * PAR
                        mm = pe.transpose(PB[4][0:rows, 40 * j + 8 * f:40 * j + 8 * f + 8], ada[:, c0:c0 + rows],
                                          ident[0:BATCH, 0:BATCH])
                mm.then_inc(adaT_mm, 1)
                pe.wait_ge(bvb_done, KT + 2)
                for t in range(KT + 1):
                    rows = PAR if t < KT else REM
                    pe.wait_ge(stage_in[t % 3], 16 * (t // 3 + 1))
                    for half in range(2):
                        mm = pe.matmul(PB[2 + half][:, 0:HALF], bvb[0:rows, t, :], stage[t % 3][0:rows, half * HALF:(half + 1) * HALF],
                                       start=(t == 0), stop=(t == KT))
                    mm.then_inc(beff_step, 1)
        stages.close()

        acts = ExitStack()
        xln = sb(acts, "xln", [PAR, TT, C])
        stats = sb(acts, "stats", [PAR, TT, 2, 6])
        mv = sb(acts, "mv", [PAR, TT, 2])
        rstd = sb(acts, "rstd", [PAR, 2, TT])
        mhalf = sb(acts, "mhalf", [PAR, TT])
        hf = [sb(acts, f"hf{i}", [PAR, TOKENS]) for i in range(2)]
        hT = sb(acts, "hT", [PAR, A_PARTS, TOKENS], fp32r)
        vv = sb(acts, "vv", [PAR, TT, HEADS, 2 * HD + 1], fp32r)
        qkhi = [sb(acts, f"qkhi{i}", [PAR, TOKENS], fp32r) for i in range(2)]
        qklo = [sb(acts, f"qklo{i}", [PAR, TOKENS], fp32r) for i in range(2)]
        qs = [sb(acts, f"qs{i}", [MROW + 1, TOKENS], fp32r) for i in range(RING)]
        ks = [sb(acts, f"ks{i}", [MROW + 1, TOKENS], fp32r) for i in range(RING)]
        negm = [sb(acts, f"negm{i}", [PAR, TT]) for i in range(2)]
        mrow = [sb(acts, f"mrow{i}", [TT, PAR], fp32r) for i in range(2)]
        phi = [sb(acts, f"phi{i}", [PAR, TOKENS], fp32r) for i in range(2)]
        plo = [sb(acts, f"plo{i}", [PAR, TOKENS], fp32r) for i in range(2)]
        ots = [sb(acts, f"ots{i}", [2 * HD + 1, TOKENS]) for i in range(2)]
        recip = [sb(acts, f"recip{i}", [PAR, TT]) for i in range(2)]
        oraw = [sb(acts, f"oraw{i}", [PAR, TT, HD]) for i in range(2)]
        early = sb(acts, "early", [PAR, TT, EARLY * HD])
        oo = sb(acts, "oo", [PAR, TT, C])
        aT = sb(acts, "aT", [PAR, A_PARTS, PAR], fp32r)
        gate = sb(acts, "gate", [PAR, C])
        xo = [sb(acts, f"xo{i}", [PAR, C]) for i in range(2)]
        ones33 = sb(acts, "ones33", [33, PAR], fp32r)

        masked = sb(acts, "masked", [RANK, 3 * RANK])
        prow = sb(acts, "prow", [RANK, 3 * RANK])
        small = sb(acts, "small", [RANK, 9])
        inv, factor, minus1, sign, placed, onehot, neg, column, pivot = (
            small[:, i:i + 1] for i in range(9))

        G, M, S, O = PB[0:2], PB[2:4], PB[4:6], PB[6]
        OW = 2 * HD + 2
        X, XM, XA = PB[7][:, 0:TT * OW], PB[7][0:TT, 0:PAR], PB[7][:, :].rearrange("p (f t) -> p f t", t=PAR)
        CONSTANTS = RING + 4

        x_in, st_done, mv_done = sem("x_in"), sem("st_done"), sem("mv_done")
        rstd_step, ln_norm, hT_hi, hT_split = sem("rstd_step"), sem("ln_norm"), sem("hT_hi"), sem("hT_split")
        g_full, g_free = sem("g_full"), sem("g_free")
        v_hi = sem("v_hi")
        qk_hi = sem("qk_hi")
        moved = {(s, p): sem(f"moved{s}{p}") for s in range(RING) for p in range(2)}
        m_full, m_read, mT, mrow_done = sem("m_full"), sem("m_read"), sem("mT"), sem("mrow_done")
        mrow_in = [sem("mrow_in0"), sem("mrow_in1")]
        s_full, exp_f, exp_hi, p_lo, pv = sem("s_full"), sem("exp_f"), sem("exp_hi"), sem("p_lo"), sem("pv")
        ot_done, oT, recip_done, o_read, o_norm = sem("ot_done"), sem("oT"), sem("recip_done"), sem("o_read"), sem("o_norm")
        early_moved = sem("early_moved")
        ax_full, ax_free = sem("ax_full"), sem("ax_free")
        a_hi = sem("a_hi")
        gate_in, r_in, xo_done, x1_out = sem("gate_in"), sem("r_in"), sem("xo_done"), sem("x1_out")
        fixed = sem("fixed")
        elim = sem("elim")

        xb = x.rearrange("b (t p) c -> b p t c", p=PAR)
        x1b = x1_d.rearrange("b (t p) c -> b p t c", p=PAR)

        def run(engine, slot):
            for b in (-1, 0):
                for n in range(SLOTS):
                    slot(b, n)
            with engine.Fori(1, BATCH - 1) as b:
                for n in range(SLOTS):
                    slot(b, n)
            for b in (BATCH - 1, BATCH):
                for n in range(SLOTS):
                    slot(b, n)

        def units(b, named):
            return [u for u in named if not isinstance(b, int) or (b, u) in G_TABLE]

        def v_use(b, half, tt):
            return g_use(b - shift(("v", half, tt)), ("v", half, tt))

        with nc.Block() as block:
            @block.sync
            def _(sp):
                for key in MOVES:
                    sp.sem_inc(moved[key], 16)
                sp.wait_ge(fixed, CONSTANTS)

                def slot(b, n):
                    for _, t in [u for u in units(b, ENDS_AT[n]) if u[0] == "qk"]:
                        bt = b + shift(("qk", t))
                        sp.wait_ge(g_free, g_use(b, ("qk", t)) + 3)
                        seen = set()
                        for h, is_k, r, rows, p0 in pieces(t):
                            if h not in seen:
                                if is_there(bt, TT * (h - RING)):
                                    sp.wait_ge(s_full, bt * SLOTS + TT * (h - RING + 1))
                                seen.add(h)
                            hi, lo = qkhi[t % 2][p0:p0 + rows, :], qklo[t % 2][p0:p0 + rows, :]
                            dst = (ks if is_k else qs)[h % RING]
                            for j, part in enumerate((hi, hi, lo) if is_k else (hi, lo, hi)):
                                sp.dma_start(f32(dst[j * HD + r:j * HD + r + rows, :]), f32(part)).then_inc(moved[h % RING, t % 2], 16)

                run(sp, slot)

            @block.gpsimd
            def _(pool):
                pool.memset(mhalf[:, :], -0.5).then_inc(fixed, 1)
                pool.memset(minus1[:, :], -1.0).then_inc(fixed, 1)
                pool.sem_inc(hT_split, 2)
                pool.sem_inc(xo_done, 2)
                pool.sem_inc(o_norm, 2)
                pool.sem_inc(elim, 1)
                pool.wait_ge(fixed, CONSTANTS)
                CHOLESKY_OPS, LU_OPS, TURN_OPS = 10, 15, 2

                def cholesky_step(k):
                    base = k * CHOLESKY_OPS
                    pool.wait_ge(elim, base + 1)
                    alone(pool)
                    pool.tensor_copy(onehot[:, :], ident[0:RANK, bass.ds(k, 1)]).then_inc(elim, 1)
                    pool.tensor_copy(neg[:, :], below[:, bass.ds(k, 1)]).then_inc(elim, 1)
                    pool.tensor_copy(column[:, :], chol[:, bass.ds(k, 1)]).then_inc(elim, 1)
                    base = base + 3
                    pool.wait_ge(elim, base + 1)
                    alone(pool)
                    pool.tensor_scalar(masked[:, :], chol[:, :], onehot[:, :], None, ALU.mult).then_inc(elim, 1)
                    pool.wait_ge(elim, base + 2)
                    alone(pool)
                    pool.partition_all_reduce(prow[:, :], masked[:, :], RANK, ADD_ALL).then_inc(elim, 1)
                    pool.tensor_tensor(dcol[:, :], dcol[:, :], masked[:, bass.ds(k, 1)], ALU.add).then_inc(elim, 1)
                    pool.wait_ge(elim, base + 4)
                    alone(pool)
                    pool.tensor_tensor(inv[:, :], prow[:, bass.ds(k, 1)], minus1[:, :], ALU.pow).then_inc(elim, 1)
                    pool.wait_ge(elim, base + 5)
                    alone(pool)
                    pool.tensor_scalar(factor[:, :], column[:, :], inv[:, :], neg[:, :], ALU.mult, ALU.mult).then_inc(elim, 1)
                    pool.wait_ge(elim, base + 6)
                    alone(pool)
                    pool.tensor_scalar(masked[:, :], prow[:, :], factor[:, :], None, ALU.mult).then_inc(elim, 1)
                    pool.wait_ge(elim, base + 7)
                    pool.tensor_tensor(chol[:, :], chol[:, :], masked[:, :], ALU.add).then_inc(elim, 1)

                def turn_to_signs():
                    base = RANK * CHOLESKY_OPS
                    pool.wait_ge(elim, base + 1)
                    pool.tensor_tensor(invroot[:, :], dcol[:, :], mhalf[0:RANK, 0:1], ALU.pow).then_inc(elim, 1)
                    pool.wait_ge(elim, base + 2)
                    alone(pool)
                    pool.tensor_scalar(lu[:, :], chol[:, 2 * RANK:3 * RANK], invroot[:, :], None, ALU.mult).then_inc(elim, 1)

                def sign_step(k):
                    base = k * LU_OPS + RANK * CHOLESKY_OPS + TURN_OPS
                    rows = masked[:, 0:RANK]
                    pool.wait_ge(elim, base + 1)
                    alone(pool)
                    pool.tensor_copy(onehot[:, :], ident[0:RANK, bass.ds(k, 1)]).then_inc(elim, 1)
                    pool.tensor_copy(neg[:, :], below[:, bass.ds(k, 1)]).then_inc(elim, 1)
                    pool.tensor_copy(column[:, :], lu[:, bass.ds(k, 1)]).then_inc(elim, 1)
                    base = base + 3
                    pool.wait_ge(elim, base + 1)
                    alone(pool)
                    pool.tensor_scalar(rows, lu[:, :], onehot[:, :], None, ALU.mult).then_inc(elim, 1)
                    pool.wait_ge(elim, base + 2)
                    alone(pool)
                    pool.partition_all_reduce(prow[:, 0:RANK], rows, RANK, ADD_ALL).then_inc(elim, 1)
                    pool.wait_ge(elim, base + 3)
                    alone(pool)
                    pool.tensor_copy(pivot[:, :], prow[:, bass.ds(k, 1)]).then_inc(elim, 1)
                    base = base + 1
                    pool.wait_ge(elim, base + 3)
                    alone(pool)
                    pool.tensor_scalar(sign[:, :], pivot[:, :], 0.0, -2.0, ALU.is_ge, ALU.mult).then_inc(elim, 1)
                    pool.wait_ge(elim, base + 4)
                    alone(pool)
                    pool.tensor_scalar(sign[:, :], sign[:, :], 1.0, None, ALU.add).then_inc(elim, 1)
                    pool.wait_ge(elim, base + 5)
                    pool.tensor_tensor(inv[:, :], pivot[:, :], sign[:, :], ALU.subtract).then_inc(elim, 1)
                    pool.wait_ge(elim, base + 6)
                    pool.tensor_tensor(inv[:, :], inv[:, :], minus1[:, :], ALU.pow).then_inc(elim, 1)
                    pool.tensor_tensor(placed[:, :], onehot[:, :], sign[:, :], ALU.mult).then_inc(elim, 1)
                    pool.wait_ge(elim, base + 8)
                    pool.tensor_tensor(scol[:, :], scol[:, :], placed[:, :], ALU.add).then_inc(elim, 1)
                    pool.tensor_scalar(factor[:, :], column[:, :], inv[:, :], neg[:, :], ALU.mult, ALU.mult).then_inc(elim, 1)
                    pool.wait_ge(elim, base + 10)
                    alone(pool)
                    pool.tensor_scalar(rows, prow[:, 0:RANK], factor[:, :], None, ALU.mult).then_inc(elim, 1)
                    pool.wait_ge(elim, base + 11)
                    pool.tensor_tensor(lu[:, :], lu[:, :], rows, ALU.add).then_inc(elim, 1)

                def load_x(b):
                    if not isinstance(b, int) or b >= 2:
                        pool.wait_ge(x1_out, 16 * TT * (b - 1))
                    pool.dma_start(xln[:, :, :].unsqueeze(1), xb[bass.ds(b, 1)].rearrange("o p t c -> p o t c")).then_inc(x_in, 16)

                def load_residual(b):
                    if isinstance(b, int) and b == BATCH - 1:
                        pool.wait_ge(x1_out, 16 * TT * b)
                    pool.dma_start(xln[:, :, :].unsqueeze(1), xb[bass.ds(b, 1)].rearrange("o p t c -> p o t c")).then_inc(r_in, 16)
                    if not isinstance(b, int) or b >= 1:
                        pool.wait_ge(g_free, g_use(b, ("p", TT - 1, 1)) + 3)
                    pool.dma_start(gate[:, :], ada_d[bass.ds(b, 1), 2 * C:3 * C].partition_broadcast(PAR)).then_inc(gate_in, 16)

                def normalise(b):
                    pool.wait_ge(mv_done, TT * (b + 1))
                    alone(pool)
                    pool.tensor_scalar(rstd[:, 0, :], mv[:, :, 1], LN_EPS, None, ALU.add).then_inc(rstd_step, 1)
                    pool.wait_ge(rstd_step, 2 * b + 1)
                    pool.tensor_tensor(rstd[:, 1, :], rstd[:, 0, :], mhalf[:, :], ALU.pow).then_inc(rstd_step, 1)
                    pool.wait_ge(rstd_step, 2 * b + 2)
                    alone(pool)
                    for tt in range(TT):
                        pool.tensor_scalar(xln[:, tt, :], xln[:, tt, :], mv[:, tt, 0:1], rstd[:, 1, tt:tt + 1],
                                           ALU.subtract, ALU.mult).then_inc(ln_norm, 1)

                def split_h(b):
                    for f in range(KT + 1):
                        rows = PAR if f < KT else REM
                        pool.wait_ge(hT_hi, (KT + 2) * b + (f + 1 if f < KT else KT + 2))
                        part = hT[0:rows, KT + f if f < KT else A_PARTS - 1, :]
                        hi = hT[0:rows, f if f < KT else 2 * KT, :]
                        pool.tensor_tensor(part, hf[f % 2][0:rows, :], f32(hi), ALU.subtract).then_inc(hT_split, 1)

                def divide(b, n):
                    h = (n // TT - 1) % HEADS
                    pool.wait_ge(o_read, b * HEADS + n // TT + 1)
                    if h < EARLY:
                        if h == 0 and (not isinstance(b, int) or b >= 1):
                            pool.wait_ge(early_moved, b)
                        head = early[:, :, h * HD:(h + 1) * HD]
                    else:
                        if h == EARLY and (not isinstance(b, int) or b >= 1):
                            pool.wait_ge(g_full, g_use(b, ("tr", TT - 1)) + 1)
                        head = oo[:, :, h * HD:(h + 1) * HD]
                    pool.tensor_tensor(head, oraw[h % 2][:, :, :], recip[h % 2][:, :].unsqueeze(2).to_broadcast([PAR, TT, HD]), ALU.mult).then_inc(o_norm, 1)

                def add_x(b, it, qt):
                    pool.wait_ge(r_in, 16 * (b + 1))
                    pool.wait_ge(g_free, g_use(it, ("p", qt, 1)) + 3)
                    pool.tensor_tensor(xln[:, qt, :], xln[:, qt, :], xo[qt % 2][:, :], ALU.add).then_inc(xo_done, 1)
                    pool.wait_ge(xo_done, b * TT + qt + 3)
                    pool.dma_start(x1b[bass.ds(b, 1), :, qt, :].rearrange("o p c -> p o c"), xln[:, qt, :].unsqueeze(1)).then_inc(x1_out, 16)

                def slot(b, n, phase):
                    inner = not isinstance(b, int)
                    if n % TT == 3 and is_there(b, n - TT):
                        divide(b, n)
                    for _, qt, half in [u for u in units(b, ENDS_AT.get(n - 3, [])) if u[0] == "p"]:
                        if half == 1:
                            add_x(b - 1, b, qt)
                    if n == LOAD_SLOT and is_there(b + 1, 0):
                        load_x(b + 1)
                    if n == NORM_SLOT and is_there(b + 1, 0):
                        normalise(b + 1)
                    if n == SPLIT_SLOT and is_there(b + 1, 0):
                        split_h(b + 1)
                    if n == RESIDUAL_SLOT and is_there(b, 0):
                        load_residual(b)
                    if n in ELIM_SLOT and is_there(b, 0):
                        (sign_step if phase else cholesky_step)((b - phase * (BATCH // 2)) * HEADS + ELIM_SLOT[n])

                for b in (-1, 0):
                    for n in range(SLOTS):
                        slot(b, n, 0)
                with pool.Fori(1, BATCH // 2) as b:
                    for n in range(SLOTS):
                        slot(b, n, 0)
                turn_to_signs()
                with pool.Fori(BATCH // 2, BATCH - 1) as b:
                    for n in range(SLOTS):
                        slot(b, n, 1)
                for b in (BATCH - 1, BATCH):
                    for n in range(SLOTS):
                        slot(b, n, 1)
                pool.wait_ge(x1_out, 16 * TT * BATCH)

            @block.scalar
            def _(act):
                act.sem_inc(ot_done, 1)
                act.sem_inc(mrow_done, 1)

                def hT_his(b, f):
                    act.wait_ge(g_free, g_use(b - 1, ("ln", f)) + 3)
                    if f < KT:
                        act.activation(hT[:, f, :], hf[f % 2][:, :], ACT.Copy).then_inc(hT_hi, 1)
                    else:
                        act.activation(hT[0:REM, 2 * KT, :], hf[f % 2][0:REM, :], ACT.Copy).then_inc(hT_hi, 1)
                        act.activation(hT[REM:PAR, 2 * KT, :], hf[f % 2][0:REM, :], ACT.Copy).then_inc(hT_hi, 1)

                def v_his(it, half, tt):
                    u = ("v", half, tt)
                    act.wait_ge(g_full, g_use(it, u) + 1)
                    act.activation(vv[:, tt, 8 * half:8 * half + 8, 0:HD], G[g_bank(it, u)][:, 0:HALF].rearrange("p (h d) -> p h d", d=HD), ACT.Copy).then_inc(v_hi, 1)

                def qk_his(it, t):
                    u = ("qk", t)
                    b = it + shift(u)
                    act.wait_ge(g_full, g_use(it, u) + 1)
                    for (ring, parity), total in MOVES.items():
                        if parity == t % 2 and total:
                            before = MOVES_AFTER[t - 2][ring, parity] if t >= 2 else 0
                            act.wait_ge(moved[ring, parity], b * (16 * total) + 16 * (before + 1))
                    act.activation(qkhi[t % 2][:, :], G[g_bank(it, u)][:, :], ACT.Identity, bias=bqk[:, t:t + 1]).then_inc(qk_hi, 1)

                def a_his(it, qt):
                    u = ("tr", qt)
                    g = g_bank(it, u)
                    act.wait_ge(ax_full, (it - 1) * TT + qt + 1)
                    act.activation(aT[:, 0:KT, :], XA, ACT.Copy).then_inc(a_hi, 1)
                    act.wait_ge(g_full, g_use(it, u) + 1)
                    act.activation(aT[0:REM, 2 * KT, :], G[g][0:REM, 0:PAR], ACT.Copy).then_inc(a_hi, 1)
                    act.activation(aT[REM:PAR, 2 * KT, :], G[g][0:REM, 0:PAR], ACT.Copy).then_inc(a_hi, 1)

                def probabilities(b, n):
                    act.wait_ge(s_full, b * SLOTS + n + 1)
                    if is_there(b, n - 2):
                        act.wait_ge(pv, b * SLOTS + n - 1)
                    act.activation(phi[n % 2][:, :], S[n % 2][:, :], ACT.Exp, scale=SCALE).then_inc(exp_hi, 1)
                    act.activation(S[n % 2][:, :], S[n % 2][:, :], ACT.Exp, scale=SCALE).then_inc(exp_f, 1)

                def take_o(b, n):
                    ho = b * HEADS + n // TT - 1
                    act.wait_ge(pv, b * SLOTS + n)
                    act.wait_ge(oT, ho + 1)
                    act.activation(ots[(n // TT - 1) % 2][:, :], O[0:2 * HD + 1, :], ACT.Copy).then_inc(ot_done, 1)

                def copy_mrow(b, h):
                    act.wait_ge(mT, b * HEADS + h + 1)
                    if is_there(b, TT * (h - 2)):
                        act.wait_ge(mrow_in[h % 2], b * (8 * HEADS) + 16 * (h // 2))
                    act.activation(mrow[h % 2][:, :], XM, ACT.Copy).then_inc(mrow_done, 1)

                def move_mrow(b, h):
                    act.wait_ge(mrow_done, b * HEADS + h + 2)
                    act.dma_start(f32(qs[h % RING][MROW:MROW + 1, :]), f32(mrow[h % 2][:, :])).then_inc(mrow_in[h % 2], 16)

                def move_early(b):
                    act.wait_ge(o_norm, b * HEADS + EARLY + 2)
                    if not isinstance(b, int) or b >= 1:
                        act.wait_ge(g_full, g_use(b, ("tr", TT - 1)) + 1)
                    act.activation(oo[:, :, 0:EARLY * HD], early[:, :, :], ACT.Copy).then_inc(early_moved, 1)

                def slot(b, n):
                    if is_there(b, n):
                        probabilities(b, n)
                    if n % TT == 0 and is_there(b, n - 1):
                        take_o(b, n)
                    if (n + 5) % TT == 0 and is_there(b, n + 5):
                        copy_mrow(b, (n + 5) // TT)
                    if (n + 4) % TT == 0 and is_there(b, n + 4):
                        move_mrow(b, (n + 4) // TT)
                    if n == EARLY_SLOT and is_there(b, 0):
                        move_early(b)
                    for u in units(b, ENDS_AT.get(n - ACT_LAG - 1, [])):
                        if u[0] == "ln":
                            hT_his(b + 1, u[1])
                    for u in units(b, ENDS_AT.get(n - ACT_LAG, [])):
                        if u[0] == "v":
                            v_his(b, u[1], u[2])
                        if u[0] == "qk":
                            qk_his(b, u[1])
                        if u[0] == "tr":
                            a_his(b, u[1])

                run(act, slot)

            @block.vector
            def _(dve):
                for i in range(RING):
                    dve.memset(f32(ks[i][:, :]), 1.0).then_inc(fixed, 1)
                dve.memset(f32(vv[:, :, :, :]), 1.0).then_inc(fixed, 1)
                dve.memset(f32(ones33[:, :]), 1.0).then_inc(fixed, 1)
                dve.sem_inc(g_free, 2)
                dve.sem_inc(m_read, 2)
                dve.sem_inc(o_read, 1)

                def statistics(b, tt):
                    if tt == 0:
                        dve.wait_ge(x_in, 16 * (b + 1))
                    for half in range(2):
                        dve.bn_stats(stats[:, tt, half, :], xln[:, tt, half * HALF:(half + 1) * HALF]).then_inc(st_done, 1)
                    dve.wait_ge(st_done, (b * TT + tt + 1) * 2)
                    alone(dve)
                    dve.bn_aggr(mv[:, tt, :], stats[:, tt, :, :]).then_inc(mv_done, 1)

                def modulate(b, f):
                    rows = PAR if f < KT else REM
                    u = ("ln", f)
                    dve.wait_ge(g_full, g_use(b - 1, u) + 1)
                    dve.wait_ge(hT_split, b * (KT + 1) + f + (1 if f else 2))
                    dve.tensor_scalar(hf[f % 2][0:rows, :], G[g_bank(b - 1, u)][0:rows, :], adaT[0:rows, 1, f, bass.ds(b, 1)],
                                      adaT[0:rows, 0, f, bass.ds(b, 1)], ALU.mult, ALU.add).then_inc(g_free, 1)

                def v_los(it, half, tt):
                    u = ("v", half, tt)
                    dve.wait_ge(v_hi, (it + shift(u)) * (2 * TT) + TT * half + tt + 1)
                    heads = vv[:, tt, 8 * half:8 * half + 8, :]
                    dve.tensor_tensor(heads[:, :, HD + 1:2 * HD + 1], G[g_bank(it, u)][:, 0:HALF].rearrange("p (h d) -> p h d", d=HD),
                                      f32(heads[:, :, 0:HD]), ALU.subtract).then_inc(g_free, 1)

                def qk_los(it, t):
                    u = ("qk", t)
                    dve.wait_ge(qk_hi, (it + shift(u)) * QK_TILES + t + 1)
                    dve.scalar_tensor_tensor(qklo[t % 2][:, :], G[g_bank(it, u)][:, :], bqk[:, t:t + 1], f32(qkhi[t % 2][:, :]),
                                             ALU.add, ALU.subtract).then_inc(g_free, 1)

                def a_los(it, qt):
                    g = g_bank(it, ("tr", qt))
                    dve.wait_ge(a_hi, 3 * ((it - 1) * TT + qt) + 1)
                    dve.tensor_tensor(aT[:, KT:2 * KT, :], XA, f32(aT[:, 0:KT, :]), ALU.subtract).then_inc(ax_free, 1)
                    dve.wait_ge(a_hi, 3 * ((it - 1) * TT + qt) + 3)
                    dve.tensor_tensor(aT[0:REM, A_PARTS - 1, :], G[g][0:REM, 0:PAR], f32(aT[0:REM, 2 * KT, :]),
                                      ALU.subtract).then_inc(g_free, 1)

                def gated(it, qt, half):
                    u = ("p", qt, half)
                    if half == 0:
                        dve.wait_ge(gate_in, 16 * it)
                        dve.wait_ge(xo_done, (it - 1) * TT + qt + 1)
                    cols = slice(half * HALF, (half + 1) * HALF)
                    dve.wait_ge(g_full, g_use(it, u) + 1)
                    dve.tensor_tensor(xo[qt % 2][:, cols], G[g_bank(it, u)][:, 0:HALF], gate[:, cols], ALU.mult).then_inc(g_free, 1)

                def row_max(b, m):
                    dve.wait_ge(m_full, b * SLOTS + m + 1)
                    if m % TT == 0 and is_there(b, m - 2 * TT):
                        dve.wait_ge(mT, b * HEADS + m // TT - 1)
                    dve.tensor_reduce(negm[m // TT % 2][:, m % TT:m % TT + 1], M[m % 2][:, :], AX.X, ALU.max, negate=True).then_inc(m_read, 1)

                def p_los(b, n):
                    dve.wait_ge(exp_f, b * SLOTS + n + 1)
                    dve.wait_ge(exp_hi, b * SLOTS + n + 1)
                    if is_there(b, n - 2):
                        dve.wait_ge(pv, b * SLOTS + n - 1)
                    dve.tensor_tensor(plo[n % 2][:, :], S[n % 2][:, :], f32(phi[n % 2][:, :]), ALU.subtract).then_inc(p_lo, 1)

                def read_o(b, n):
                    ho, i = b * HEADS + n // TT - 1, (n // TT - 1) % 2
                    view = X.rearrange("p (t c) -> p t c", c=OW)
                    dve.wait_ge(oT, ho + 3)
                    dve.wait_ge(o_norm, ho + 1)
                    dve.reciprocal(recip[i][:, :], view[:, :, HD]).then_inc(recip_done, 1)
                    pair = view[:, :, 0:2 * (HD + 1)].rearrange("p t (two d) -> p t d two", two=2)[:, :, 0:HD, :]
                    dve.wait_ge(recip_done, ho + 1)
                    dve.tensor_reduce(oraw[i][:, :, :], pair, AX.X, ALU.add).then_inc(o_read, 1)

                def slot(b, n):
                    if is_there(b, n):
                        p_los(b, n)
                    if is_there(b, n + MAX_LEAD - 1):
                        row_max(b, n + MAX_LEAD - 1)
                    for u in units(b, ENDS_AT.get(n - DVE_LAG, [])):
                        if u[0] == "ln":
                            modulate(b + 1, u[1])
                        if u[0] == "v":
                            v_los(b, u[1], u[2])
                        if u[0] == "qk":
                            qk_los(b, u[1])
                        if u[0] == "tr":
                            a_los(b, u[1])
                        if u[0] == "p":
                            gated(b, u[1], u[2])
                    if n % TT == 2 and is_there(b, n - TT):
                        read_o(b, n)
                    if STAT_SLOT <= n < STAT_SLOT + TT and is_there(b + 1, 0):
                        statistics(b + 1, n - STAT_SLOT)

                run(dve, slot)

            @block.tensor
            def _(pe):
                pe.sem_inc(oT, 2)
                pe.wait_ge(fixed, CONSTANTS)

                def halves(part, passes):
                    middle = len(passes) // 2
                    for j in range(*((0, middle) if part == 0 else (middle, len(passes)))):
                        yield passes[j], j == 0, j == len(passes) - 1

                def transpose_x(it, f):
                    rows = PAR if f < KT else REM
                    u = ("ln", f)
                    pe.wait_ge(g_free, g_use(it, u) + 1)
                    alone(pe)
                    for tt in range(TT):
                        if f == 0:
                            pe.wait_ge(ln_norm, (it + 1) * TT + tt + 1)
                        mm = pe.transpose(G[g_bank(it, u)][0:rows, tt * PAR:(tt + 1) * PAR], xln[:, tt, f * PAR:f * PAR + rows], ident[:, :])
                    mm.then_inc(g_full, 1)

                def v_tile(it, half, tt, part):
                    u = ("v", half, tt)
                    if part == 0:
                        if half == 0 and tt == 0:
                            pe.wait_ge(hT_split, (it + 2) * (KT + 1) + 2)
                        pe.wait_ge(g_free, g_use(it, u) + 1)
                    for (w, a, rows), first, last in halves(part, PASSES):
                        mm = pe.matmul(G[g_bank(it, u)][:, 0:HALF], hT[0:rows, a, tt * PAR:(tt + 1) * PAR],
                                       wv[0:rows, w, half * HALF:(half + 1) * HALF], start=first, stop=last)
                    if part == 1:
                        mm.then_inc(g_full, 1)

                def qk_tile(it, t, part):
                    u = ("qk", t)
                    if part == 0:
                        pe.wait_ge(g_free, g_use(it, u) + 1)
                    for (w, a, rows), first, last in halves(part, PASSES):
                        mm = pe.matmul(G[g_bank(it, u)][:, :], wqk[0:rows, w, t * PAR:(t + 1) * PAR], hT[0:rows, a, :],
                                       start=first, stop=last)
                    if part == 1:
                        mm.then_inc(g_full, 1)

                def transpose_out(it, qt):
                    u = ("tr", qt)
                    g = g_bank(it, u)
                    if qt == 0:
                        pe.wait_ge(o_norm, it * HEADS + 2)
                        pe.wait_ge(early_moved, it)
                    pe.wait_ge(o_read, it * HEADS + (TR_SLOT[qt] // TT + 1 if is_there(it, 0) else 1))
                    if is_there(it, TR_SLOT[qt] + 5):
                        pe.wait_ge(mrow_done, it * HEADS + (TR_SLOT[qt] + 5) // TT + 2)
                    for f in range(KT):
                        mm = pe.transpose(XA[:, f, :], oo[:, qt, f * PAR:(f + 1) * PAR], ident[:, :])
                    mm.then_inc(ax_full, 1)
                    pe.wait_ge(g_free, g_use(it, u) + 1)
                    alone(pe)
                    pe.transpose(G[g][0:REM, 0:PAR], oo[:, qt, KT * PAR:C], ident[:, :]).then_inc(g_full, 1)

                def project(it, qt, half, part):
                    u = ("p", qt, half)
                    cols = slice(half * HALF, (half + 1) * HALF)
                    bank = G[g_bank(it, u)][:, 0:HALF]
                    if part == 0:
                        pe.wait_ge(g_free, g_use(it, u) + 1)
                        if half == 0:
                            pe.wait_ge(ax_free, (it - 1) * TT + qt + 1)
                            pe.wait_ge(g_free, g_use(it, ("tr", qt)) + 3)
                        pe.matmul(bank, ones33[:, :], bias2[:, cols], start=True, stop=False)
                    for (w, a, rows), _, last in halves(part, PASSES):
                        mm = pe.matmul(bank, aT[0:rows, a, :], wp[0:rows, w, cols], start=False, stop=last)
                    if part == 1:
                        mm.then_inc(g_full, 1)

                def scores_for_max(b, m):
                    h, bm = m // TT % HEADS, b + m // SLOTS
                    if m % TT == 0:
                        for (ring, parity), total in MOVES.items():
                            count = MOVES_AFTER[last_tile(h)][ring, parity]
                            if ring == h % RING and count:
                                pe.wait_ge(moved[ring, parity], bm * (16 * total) + 16 * (count + 1))
                    pe.wait_ge(m_read, b * SLOTS + m + 1)
                    qt = m % TT
                    pe.matmul(M[m % 2][:, :], qs[h % RING][0:STACK, qt * PAR:(qt + 1) * PAR], ks[h % RING][0:STACK, :],
                              start=True, stop=True).then_inc(m_full, 1)

                def transpose_max(b, h):
                    pe.wait_ge(m_read, b * SLOTS + TT * (h + 1) + 2)
                    pe.wait_ge(mrow_done, b * HEADS + h + 1)
                    if is_there(b, TT * (h - 3)):
                        pe.wait_ge(o_read, b * HEADS + h - 1)
                    pe.transpose(XM, negm[h % 2][:, :], ident[:, :]).then_inc(mT, 1)

                def scores(b, m):
                    h, kt = m // TT % HEADS, m % TT
                    if kt == 0:
                        pe.wait_ge(mrow_in[h % 2], b * (8 * HEADS) + 16 * (m // TT // 2 + 1))
                    if is_there(b, m - 2):
                        pe.wait_ge(p_lo, b * SLOTS + m - 1)
                    pe.matmul(S[m % 2][:, :], ks[h % RING][:, kt * PAR:(kt + 1) * PAR], qs[h % RING][:, :],
                              start=True, stop=True).then_inc(s_full, 1)

                def values(b, n):
                    h, kt = n // TT, n % TT
                    if kt == 0:
                        pe.wait_ge(ot_done, b * HEADS + h + 1)
                    if h % 8 == 0:
                        pe.wait_ge(g_free, v_use(b, h // 8, kt) + 3)
                    pe.wait_ge(p_lo, b * SLOTS + n + 1)
                    v = vv[:, kt, h, 0:2 * HD + 1]
                    pe.matmul(O[0:2 * HD + 1, :], v, phi[n % 2][:, :], start=(kt == 0), stop=False)
                    pe.matmul(O[0:2 * HD + 1, :], v, plo[n % 2][:, :], start=False, stop=(kt == TT - 1)).then_inc(pv, 1)

                def transpose_o(b, n):
                    ho, i = b * HEADS + n // TT - 1, (n // TT - 1) % 2
                    pe.wait_ge(ot_done, ho + 2)
                    pe.wait_ge(o_read, ho + 1)
                    if is_there(b, n + 3):
                        pe.wait_ge(mrow_done, b * HEADS + (n + 3) // TT + 2)
                    for _, qt in [u for u in units(b, ENDS_AT[n - 2] if n > 1 else []) if u[0] == "tr"]:
                        pe.wait_ge(ax_free, (b - 1) * TT + qt + 1)
                    for qt in range(TT):
                        mm = pe.transpose(X[:, qt * OW:qt * OW + 2 * HD + 1], ots[i][:, qt * PAR:(qt + 1) * PAR],
                                          ident[0:2 * HD + 1, 0:2 * HD + 1])
                    mm.then_inc(oT, 1)

                def slot(b, n):
                    if is_there(b, n + MAX_LEAD):
                        scores_for_max(b, n + MAX_LEAD)
                    if (n + 5) % TT == 0 and is_there(b, n + 5):
                        transpose_max(b, (n + 5) // TT)
                    if n % TT == 1 and is_there(b, n - TT):
                        transpose_o(b, n)
                    for u, part in PARTS_AT[n]:
                        if not units(b, [u]):
                            continue
                        if u[0] == "ln":
                            transpose_x(b, u[1])
                        if u[0] == "v":
                            v_tile(b, u[1], u[2], part)
                        if u[0] == "qk":
                            qk_tile(b, u[1], part)
                        if u[0] == "tr":
                            transpose_out(b, u[1])
                        if u[0] == "p":
                            project(b, u[1], u[2], part)
                    if is_there(b, n):
                        values(b, n)
                    if is_there(b, n + 2):
                        scores(b, n + 2)

                run(pe, slot)
        acts.close()
        attn.close()

        FT = FF // PAR
        w1 = sb(every, "w1", [PAR, W_PARTS, FF], fp32r)
        w2 = sb(every, "w2", [PAR, FT, 2, C], fp32r)
        b1 = sb(every, "b1", [PAR, FT])
        UT = sb(every, "UT", [RANK, C])
        rot = ExitStack()
        VC = 128
        NV = RANK * RANK // VC
        wr = [sb(rot, f"wr{i}", [PAR, KT + 1, VC]) for i in range(2)]
        brc = [sb(rot, f"brc{i}", [BATCH, VC]) for i in range(2)]
        vrow = [sb(rot, f"vrow{i}", [BATCH, VC]) for i in range(2)]
        wst = [sb(rot, f"wst{i}", [PAR, C]) for i in range(3)]
        SQ = [RANK, BATCH, RANK]
        skew, nskew, y1, y2, y3 = (sb(rot, n, SQ) for n in ("skew", "nskew", "y1", "y2", "y3"))
        ev, od, R, RT = (sb(rot, n, SQ) for n in ("ev", "od", "R", "RT"))
        over = sb(rot, "over", [RANK, SQUARINGS, BATCH])
        take = sb(rot, "take", [RANK, BATCH])
        half_of = sb(rot, "half_of", [RANK, SQUARINGS, BATCH])
        sq_sum = sb(rot, "sq_sum", [RANK, BATCH])
        frob = sb(rot, "frob", [RANK, BATCH])
        ones64 = sb(rot, "ones64", [RANK, RANK])
        upper = sb(rot, "upper", [RANK, RANK])
        linvT = sb(rot, "linvT", [RANK, RANK])
        su = sb(rot, "su", [RANK, 1])
        prows = sb(rot, "prows", [RANK, C])
        esb = [sb(rot, f"esb{i}", [PAR, BATCH, RANK]) for i in range(2)]
        eye8 = prows[:, 0:BATCH * RANK].rearrange("p (b j) -> p b j", j=RANK)

        wr_in, brc_in = [sem("wr_in0"), sem("wr_in1")], [sem("brc_in0"), sem("brc_in1")]
        vmm, vrow_done, vrow_out = sem("vmm"), sem("vrow_done"), [sem("vrow_out0"), sem("vrow_out1")]
        skew_in, prows_in, ones_set = sem("skew_in"), sem("prows_in"), sem("ones_set")
        rmm, rstep, sq_mm, sq_done = sem("rmm"), sem("rstep"), sem("sq_mm"), sem("sq_done")
        linv_mm, linv_done, ut_mm, ut_done = sem("linv_mm"), sem("linv_done"), sem("ut_mm"), sem("ut_done")
        e_mm, e_done, e_out = sem("e_mm"), sem("e_done"), [sem("e_out0"), sem("e_out1")]
        wst_in, whi, wlo = [sem(f"wst_in{i}") for i in range(3)], sem("whi"), sem("wlo")
        b1_in, rmm_in, over_set, take_set = sem("b1_in"), sem("rmm_in"), sem("over_set"), sem("take_set")

        WS = []
        for q in range(FF // C):
            cols = slice(q * C, (q + 1) * C)
            for t in range(KT + 1):
                if t < KT:
                    WS.append((w_fc1[t * PAR:(t + 1) * PAR, cols], w1[:, t, cols], w1[:, KT + t, cols], PAR))
                else:
                    WS.append((w_fc1[KT * PAR:C, cols], w1[0:REM, 2 * KT, cols], w1[REM:PAR, 2 * KT, cols], REM))
        for t in range(FT):
            WS.append((w_fc2[t * PAR:(t + 1) * PAR, :], w2[:, t, 0, :], w2[:, t, 1, :], PAR))

        def flat(m):
            return m[:, :, :].rearrange("p b j -> p (b j)")

        with nc.Block() as block:
            @block.sync
            def _(sp):
                sp.dma_start(prows[:, :], p_rows).then_inc(prows_in, 16)
                sp.dma_start(b1[:, :], b_fc1).then_inc(b1_in, 16)
                for v in range(NV):
                    cols = slice(v * VC, (v + 1) * VC)
                    if v >= 2:
                        sp.wait_ge(vmm, v - 1)
                        sp.wait_ge(vrow_done, v - 1)
                    sp.dma_start(wr[v % 2][:, 0:KT, :], w_rot[0:KT * PAR, cols].rearrange("(k p) n -> p k n", p=PAR)).then_inc(wr_in[v % 2], 16)
                    sp.dma_start(wr[v % 2][0:REM, KT, :], w_rot[KT * PAR:C, cols]).then_inc(wr_in[v % 2], 16)
                    sp.dma_start(brc[v % 2][:, :], b_rot[:, cols].partition_broadcast(BATCH)).then_inc(brc_in[v % 2], 16)
                    if v >= 1:
                        sp.wait_ge(vrow_done, v)
                        sp.dma_start(rot_d[:, (v - 1) * VC:v * VC], vrow[(v - 1) % 2][:, :]).then_inc(vrow_out[(v - 1) % 2], 16)
                sp.wait_ge(vrow_done, NV)
                sp.dma_start(rot_d[:, (NV - 1) * VC:NV * VC], vrow[(NV - 1) % 2][:, :]).then_inc(vrow_out[(NV - 1) % 2], 16)
                for p in range(2):
                    sp.wait_ge(vrow_out[p], 16 * (NV // 2))
                sp.dma_start(skew[:, :, :], rot_d.rearrange("b (i j) -> i b j", j=RANK)).then_inc(skew_in, 16)
                for n, (src, hi, lo, rows) in enumerate(WS):
                    if n >= 3:
                        sp.wait_ge(wlo, n - 2)
                    sp.dma_start(wst[n % 3][0:rows, :], src).then_inc(wst_in[n % 3], 16)
                for f in range(KT + 1):
                    rows = PAR if f < KT else REM
                    sp.wait_ge(e_done, f + 1)
                    sp.dma_start(e_d[:, 0:rows, f * RANK:(f + 1) * RANK].rearrange("b p e -> p b e"), esb[f % 2][0:rows, :, :]).then_inc(e_out[f % 2], 16)
                for p in range(2):
                    sp.wait_ge(e_out[p], 16 * (3 - p))
                sp.wait_ge(b1_in, 16)

            @block.gpsimd
            def _(pool):
                for n, (src, hi, lo, rows) in enumerate(WS):
                    pool.wait_ge(whi, n + 1)
                    if n:
                        pool.wait_ge(wlo, n)
                    pool.tensor_tensor(lo, wst[n % 3][0:rows, :], f32(hi), ALU.subtract).then_inc(wlo, 1)

            @block.scalar
            def _(act):
                for n, (src, hi, lo, rows) in enumerate(WS):
                    act.wait_ge(wst_in[n % 3], 16 * (n // 3 + 1))
                    act.activation(hi, wst[n % 3][0:rows, :], ACT.Copy).then_inc(whi, 1)

            @block.vector
            def _(dve):
                done = [0]

                def step(ins):
                    done[0] += 1
                    ins.then_inc(rstep, 1)
                    dve.wait_ge(rstep, done[0])

                step(dve.memset(ones64[:, :], 1.0))
                step(dve.tensor_scalar(upper[:, :], below[:, :], 2.0, 1.0, ALU.mult, ALU.add))
                step(dve.tensor_tensor(su[:, :], scol[:, :], invroot[:, :], ALU.mult))
                dve.wait_ge(linv_mm, 1)
                dve.tensor_copy(linvT[:, :], PB[2][0:RANK, 0:RANK]).then_inc(linv_done, 1)
                dve.wait_ge(ut_mm, 1)
                for half in range(2):
                    dve.tensor_scalar(UT[:, half * HALF:(half + 1) * HALF], PB[3 + half][0:RANK, 0:HALF], su[:, 0:1], None, ALU.mult).then_inc(ut_done, 1)
                for v in range(NV):
                    dve.wait_ge(vmm, v + 1)
                    dve.wait_ge(brc_in[v % 2], 16 * (v // 2 + 1))
                    if v >= 2:
                        dve.wait_ge(vrow_out[v % 2], 16 * (v // 2))
                    dve.tensor_tensor(vrow[v % 2][:, :], PB[v % 2][0:BATCH, 0:VC], brc[v % 2][:, :], ALU.add).then_inc(vrow_done, 1)
                dve.wait_ge(skew_in, 16)
                step(dve.tensor_tensor(skew[:, :, :], skew[:, :, :], upper[:, :].unsqueeze(1).to_broadcast(SQ), ALU.mult))
                step(dve.tensor_tensor(y1[:, :, :], skew[:, :, :], skew[:, :, :], ALU.mult))
                dve.tensor_reduce(sq_sum[:, :], y1[:, :, :], AX.X, ALU.add).then_inc(rmm_in, 1)
                dve.wait_ge(rmm, 1)
                step(dve.tensor_copy(frob[:, :], PB[5][0:RANK, 0:BATCH]))
                for k in range(SQUARINGS):
                    dve.tensor_scalar(over[:, k, :], frob[:, :], 4.0 * 4.0 ** k, None, ALU.is_gt).then_inc(over_set, 1)
                dve.wait_ge(over_set, SQUARINGS)
                step(dve.tensor_scalar(half_of[:, :, :], over[:, :, :], -0.5, 1.0, ALU.mult, ALU.add))
                n = SQUARINGS
                while n > 1:
                    n //= 2
                    step(dve.tensor_tensor(half_of[:, 0:n, :], half_of[:, 0:n, :], half_of[:, n:2 * n, :], ALU.mult))
                step(dve.tensor_tensor(skew[:, :, :], skew[:, :, :], half_of[:, 0, :].unsqueeze(2).to_broadcast(SQ), ALU.mult))
                dve.tensor_scalar(nskew[:, :, :], skew[:, :, :], -1.0, None, ALU.mult).then_inc(rmm_in, 1)
                for n, y in enumerate((y1, y2, y3)):
                    dve.wait_ge(rmm, n + 2)
                    dve.tensor_copy(flat(y), PB[5][0:RANK, :]).then_inc(rmm_in, 1)
                eye = ident[0:RANK, 0:RANK].unsqueeze(1).to_broadcast(SQ)
                c = TAYLOR
                dve.wait_ge(rmm_in, 5)

                def series(out, c0, c1, c2, c3):
                    step(dve.tensor_scalar(flat(out), flat(y1), c1, None, ALU.mult))
                    step(dve.scalar_tensor_tensor(out=flat(out), in0=flat(y2), scalar=c2, in1=flat(out), op0=ALU.mult, op1=ALU.add))
                    if c3:
                        step(dve.scalar_tensor_tensor(out=flat(out), in0=flat(y3), scalar=c3, in1=flat(out), op0=ALU.mult, op1=ALU.add))
                    step(dve.tensor_scalar(flat(RT), diag8(), c0, None, ALU.mult))
                    step(dve.tensor_tensor(flat(out), flat(out), flat(RT), ALU.add))

                def diag8():
                    return flat(eye8)

                step(dve.tensor_copy(eye8[:, :, :], eye))
                series(ev, c[6], c[8], c[10], c[12])
                series(od, c[7], c[9], c[11], 0.0)
                dve.tensor_copy(flat(R), flat(ev)).then_inc(rmm_in, 1)
                dve.wait_ge(rmm, 6)
                series(ev, c[0], c[2], c[4], 0.0)
                step(dve.tensor_tensor(flat(ev), flat(ev), PB[6][0:RANK, :], ALU.add))
                step(dve.tensor_copy(flat(R), flat(od)))
                series(od, c[1], c[3], c[5], 0.0)
                dve.tensor_tensor(flat(od), flat(od), PB[7][0:RANK, :], ALU.add).then_inc(rmm_in, 1)
                dve.wait_ge(rmm, 7)
                dve.tensor_tensor(flat(R), flat(ev), PB[5][0:RANK, :], ALU.add).then_inc(sq_done, 1)
                dve.tensor_tensor(flat(RT), flat(ev), PB[5][0:RANK, :], ALU.subtract).then_inc(sq_done, 1)
                with dve.Fori(0, SQUARINGS) as k:
                    dve.wait_ge(sq_done, 2 * k + 2)
                    dve.tensor_copy(take[:, :], over[:, bass.ds(k, 1), :].rearrange("p o b -> p (o b)")).then_inc(take_set, 1)
                    took = take[:, :].unsqueeze(2).to_broadcast(SQ).bitcast(mybir.dt.uint32)
                    dve.wait_ge(take_set, k + 1)
                    dve.wait_ge(sq_mm, 2 * k + 2)
                    alone(dve)
                    dve.copy_predicated(R[:, :, :], took, PB[0][0:RANK, :].rearrange("p (b j) -> p b j", j=RANK)).then_inc(sq_done, 1)
                    dve.copy_predicated(RT[:, :, :], took, PB[1][0:RANK, :].rearrange("p (b j) -> p b j", j=RANK)).then_inc(sq_done, 1)
                dve.wait_ge(sq_done, 2 * SQUARINGS + 2)
                dve.tensor_tensor(flat(R), flat(R), flat(eye8), ALU.subtract).then_inc(sq_done, 1)
                for f in range(KT + 1):
                    rows = PAR if f < KT else REM
                    dve.wait_ge(e_mm, f + 1)
                    if f >= 2:
                        dve.wait_ge(e_out[f % 2], 16 * (f // 2))
                    dve.tensor_copy(flat(esb[f % 2])[0:rows, :], PB[2 + f % 2][0:rows, :]).then_inc(e_done, 1)

            @block.tensor
            def _(pe):
                pe.transpose(PB[2][0:RANK, 0:RANK], chol[:, RANK:2 * RANK], ident[0:RANK, 0:RANK]).then_inc(linv_mm, 1)
                pe.wait_ge(linv_done, 1)
                pe.wait_ge(prows_in, 16)
                for half in range(2):
                    mm = pe.matmul(PB[3 + half][0:RANK, 0:HALF], linvT[:, :], prows[:, half * HALF:(half + 1) * HALF], start=True, stop=True)
                mm.then_inc(ut_mm, 1)
                for v in range(NV):
                    pe.wait_ge(wr_in[v % 2], 32 * (v // 2 + 1))
                    if v >= 2:
                        pe.wait_ge(vrow_done, v - 1)
                    for t in range(KT + 1):
                        rows = PAR if t < KT else REM
                        mm = pe.matmul(PB[v % 2][0:BATCH, 0:VC], siluT[0:rows, t, :], wr[v % 2][0:rows, t, :], start=(t == 0), stop=(t == KT))
                    mm.then_inc(vmm, 1)

                def products(bank, left, right, done):
                    for b in range(BATCH):
                        mm = pe.matmul(bank[0:RANK, b * RANK:(b + 1) * RANK], left[:, b, :], right[:, b, :], start=True, stop=True)
                    if done is not None:
                        mm.then_inc(done, 1)

                pe.wait_ge(rmm_in, 1)
                pe.matmul(PB[5][0:RANK, 0:BATCH], ones64[:, :], sq_sum[:, :], start=True, stop=True).then_inc(rmm, 1)
                pe.wait_ge(rmm_in, 2)
                products(PB[5], nskew, skew, rmm)
                pe.wait_ge(rmm_in, 3)
                products(PB[5], y1, y1, rmm)
                pe.wait_ge(rmm_in, 4)
                products(PB[5], y1, y2, rmm)
                pe.wait_ge(rmm_in, 6)
                products(PB[6], y3, R, rmm)
                products(PB[7], y3, od, rmm)
                pe.wait_ge(rmm_in, 7)
                products(PB[5], nskew, od, rmm)
                with pe.Fori(0, SQUARINGS) as k:
                    pe.wait_ge(sq_done, 2 * k + 2)
                    alone(pe)
                    products(PB[0], RT, R, sq_mm)
                    products(PB[1], R, RT, sq_mm)
                pe.wait_ge(sq_done, 2 * SQUARINGS + 3)
                pe.wait_ge(ut_done, 2)
                for f in range(KT + 1):
                    rows = PAR if f < KT else REM
                    if f >= 2:
                        pe.wait_ge(e_done, f - 1)
                    pe.matmul(PB[2 + f % 2][0:rows, :], UT[:, f * PAR:f * PAR + rows], flat(R), start=True, stop=True).then_inc(e_mm, 1)
        rot.close()

        CH = 2 * PAR
        CT, NC = CH // PAR, TOKENS // CH
        mlp = ExitStack()
        every.enter_context(mlp)
        xa = sb(mlp, "xa", [PAR, CT, C])
        xs = sb(mlp, "xs", [PAR, CT, C])
        stats2 = sb(mlp, "stats2", [PAR, CT, 2, 6])
        mv2 = sb(mlp, "mv2", [PAR, CT, 2])
        rstd2 = sb(mlp, "rstd2", [PAR, 2, CT])
        mhalf2 = sb(mlp, "mhalf2", [PAR, CT])
        hg = [sb(mlp, f"hg{i}", [PAR, CH]) for i in range(2)]
        h2T = sb(mlp, "h2T", [PAR, A_PARTS, CH], fp32r)
        gf = [sb(mlp, f"gf{i}", [PAR, CH]) for i in range(2)]
        ghi = [sb(mlp, f"ghi{i}", [PAR, CH], fp32r) for i in range(2)]
        glo = [sb(mlp, f"glo{i}", [PAR, CH], fp32r) for i in range(2)]
        x2T = sb(mlp, "x2T", [PAR, KT + 1, CH])
        dzT = sb(mlp, "dzT", [RANK, CH])
        ecur = sb(mlp, "ecur", [PAR, KT + 1, RANK])
        gate2 = sb(mlp, "gate2", [PAR, C])
        gb2 = sb(mlp, "gb2", [PAR, C])
        tmp = sb(mlp, "tmp", [PAR, HALF])

        Y, F, G = PB[0:4], PB[4:6], PB[6:8]
        H_LN, H_X2, H_Z, H_OUT = 0, KT + 1, 2 * (KT + 1), 2 * (KT + 1) + 1
        H_ALL = H_OUT + 2 * CT
        xa_in, xs_in, xs_out = sem("xa_in"), sem("xs_in"), sem("xs_out")
        st2, mv2_done, rstd2_step, ln2, h_hi, h_split = sem("st2"), sem("mv2_done"), sem("rstd2_step"), sem("ln2"), sem("h_hi"), sem("h_split")
        k_full, k_free = sem("k_full"), sem("k_free")
        f_full, gelu_f, gelu_hi, g_lo, fc2_mm, y_full, y_read = (sem(n) for n in ("f_full", "gelu_f", "gelu_hi", "g_lo", "fc2_mm", "y_full", "y_read"))
        gate2_in, e_in, gb2_done, xs_biased, x2_done, x2T_done, dz_done, out_done = (sem(n) for n in ("gate2_in", "e_in", "gb2_done", "xs_biased", "x2_done", "x2T_done", "dz_done", "out_done"))
        fixed2 = sem("fixed2")
        x1c = x1_d.rearrange("b (t p) c -> b p t c", p=PAR)
        outc = out.rearrange("b (t p) c -> b p t c", p=PAR)

        with nc.Block() as block:
            @block.sync
            def _(sp):
                sp.sem_inc(xs_out, 16)
                with sp.Fori(0, BATCH) as b:
                    for j in range(NC):
                        n = b * NC + j
                        span = slice(j * CT, (j + 1) * CT)
                        sp.wait_ge(xs_out, 16 * (n + 1))
                        sp.dma_start(xs[:, :, :].unsqueeze(1), x1c[bass.ds(b, 1), :, span, :].rearrange("o p t c -> p o t c")).then_inc(xs_in, 16)
                        sp.wait_ge(k_free, n * H_ALL + 2)
                        sp.dma_start(xa[:, :, :].unsqueeze(1), x1c[bass.ds(b, 1), :, span, :].rearrange("o p t c -> p o t c")).then_inc(xa_in, 16)
                        if j == 0:
                            sp.dma_start(gate2[:, :], ada_d[bass.ds(b, 1), 5 * C:6 * C].partition_broadcast(PAR)).then_inc(gate2_in, 16)
                            sp.wait_ge(gb2_done, 2 * b + 1)
                            sp.dma_start(gb2[:, :], b_fc2.partition_broadcast(PAR)).then_inc(gate2_in, 16)
                            sp.dma_start(ecur[:, 0:KT, :].unsqueeze(1), e_d[bass.ds(b, 1), :, 0:KT * RANK].rearrange("o p (f e) -> p o f e", e=RANK)).then_inc(e_in, 16)
                            sp.dma_start(ecur[0:REM, KT, :].unsqueeze(1), e_d[bass.ds(b, 1), 0:REM, KT * RANK:(KT + 1) * RANK].rearrange("o p e -> p o e")).then_inc(e_in, 16)
                        sp.wait_ge(out_done, 2 * CT * (n + 1))
                        sp.dma_start(outc[bass.ds(b, 1), :, span, :].rearrange("o p t c -> p o t c"), xs[:, :, :].unsqueeze(1)).then_inc(xs_out, 16)
                sp.wait_ge(xs_out, 16 * (BATCH * NC + 1))

            @block.gpsimd
            def _(pool):
                pool.memset(mhalf2[:, :], -0.5).then_inc(fixed2, 1)
                pool.wait_ge(fixed2, 1)
                pool.sem_inc(h_split, 2)
                pool.sem_inc(gb2_done, 1)
                with pool.Fori(0, BATCH) as b:
                    for j in range(NC):
                        n = b * NC + j
                        pool.wait_ge(mv2_done, CT * (n + 1))
                        alone(pool)
                        pool.tensor_scalar(rstd2[:, 0, :], mv2[:, :, 1], LN_EPS, None, ALU.add).then_inc(rstd2_step, 1)
                        pool.wait_ge(rstd2_step, 2 * n + 1)
                        pool.tensor_tensor(rstd2[:, 1, :], rstd2[:, 0, :], mhalf2[:, :], ALU.pow).then_inc(rstd2_step, 1)
                        pool.wait_ge(rstd2_step, 2 * n + 2)
                        alone(pool)
                        for tt in range(CT):
                            pool.tensor_scalar(xa[:, tt, :], xa[:, tt, :], mv2[:, tt, 0:1], rstd2[:, 1, tt:tt + 1],
                                               ALU.subtract, ALU.mult).then_inc(ln2, 1)
                        for f in range(KT + 1):
                            rows = PAR if f < KT else REM
                            pool.wait_ge(h_hi, (KT + 2) * n + (f + 1 if f < KT else KT + 2))
                            part = h2T[0:rows, KT + f if f < KT else A_PARTS - 1, :]
                            hi = h2T[0:rows, f if f < KT else 2 * KT, :]
                            pool.tensor_tensor(part, hg[(5 * j + f) % 2][0:rows, :], f32(hi), ALU.subtract).then_inc(h_split, 1)
                        if j == 0:
                            pool.wait_ge(gate2_in, 32 * (b + 1))
                            pool.tensor_tensor(gb2[:, :], gate2[:, :], gb2[:, :], ALU.mult).then_inc(gb2_done, 1)
                            pool.wait_ge(gb2_done, 2 * b + 2)
                        pool.wait_ge(xs_in, 16 * (n + 1))
                        for tt in range(CT):
                            last = pool.tensor_tensor(xs[:, tt, :], xs[:, tt, :], gb2[:, :], ALU.add)
                            last.then_inc(xs_biased, 1)
                        if j == NC - 1:
                            pool.wait_ge(xs_biased, CT * (n + 1))
                            pool.sem_inc(gb2_done, 1)

            @block.scalar
            def _(act):
                act.sem_inc(gelu_hi, 2)
                with act.Fori(0, BATCH) as b:
                    for j in range(NC):
                        n = b * NC + j
                        for f in range(KT + 1):
                            src = hg[(5 * j + f) % 2]
                            act.wait_ge(k_free, n * H_ALL + H_LN + f + 3)
                            if f < KT:
                                act.activation(h2T[:, f, :], src[:, :], ACT.Copy).then_inc(h_hi, 1)
                            else:
                                act.activation(h2T[0:REM, 2 * KT, :], src[0:REM, :], ACT.Copy).then_inc(h_hi, 1)
                                act.activation(h2T[REM:PAR, 2 * KT, :], src[0:REM, :], ACT.Copy).then_inc(h_hi, 1)
                        for ft in range(FT):
                            m = n * FT + ft
                            act.wait_ge(f_full, m + 1)
                            act.wait_ge(g_lo, m + 1)
                            act.activation(gf[ft % 2][:, :], F[ft % 2][:, 0:CH], ACT.Gelu_apprx_tanh, bias=b1[:, ft:ft + 1]).then_inc(gelu_f, 1)
                            act.wait_ge(fc2_mm, m + 1)
                            act.activation(ghi[ft % 2][:, :], F[ft % 2][:, 0:CH], ACT.Gelu_apprx_tanh, bias=b1[:, ft:ft + 1]).then_inc(gelu_hi, 1)
                        for f in range(KT + 1):
                            rows = PAR if f < KT else REM
                            g = H_X2 + f
                            act.wait_ge(k_full, n * H_ALL + g + 1)
                            act.activation(x2T[0:rows, f, :], G[(j * H_ALL + g) % 2][0:rows, 0:CH], ACT.Copy).then_inc(x2T_done, 1)
                        act.wait_ge(k_full, n * H_ALL + H_Z + 1)
                        act.activation(dzT[:, :], G[(j * H_ALL + H_Z) % 2][0:RANK, 0:CH], ACT.Copy).then_inc(dz_done, 1)

            @block.vector
            def _(dve):
                dve.sem_inc(g_lo, 2)
                dve.sem_inc(k_free, 2)
                dve.sem_inc(y_read, 1)
                with dve.Fori(0, BATCH) as b:
                    for j in range(NC):
                        n = b * NC + j
                        dve.wait_ge(xa_in, 16 * (n + 1))
                        for tt in range(CT):
                            for half in range(2):
                                dve.bn_stats(stats2[:, tt, half, :], xa[:, tt, half * HALF:(half + 1) * HALF]).then_inc(st2, 1)
                            dve.wait_ge(st2, (n * CT + tt + 1) * 2)
                            alone(dve)
                            dve.bn_aggr(mv2[:, tt, :], stats2[:, tt, :, :]).then_inc(mv2_done, 1)
                        for f in range(KT + 1):
                            rows = PAR if f < KT else REM
                            g = H_LN + f
                            dve.wait_ge(k_full, n * H_ALL + g + 1)
                            dve.wait_ge(h_split, n * (KT + 1) + f + 1)
                            dve.tensor_scalar(hg[(5 * j + f) % 2][0:rows, :], G[(j * H_ALL + g) % 2][0:rows, 0:CH], adaT[0:rows, 3, f, bass.ds(b, 1)],
                                              adaT[0:rows, 2, f, bass.ds(b, 1)], ALU.mult, ALU.add).then_inc(k_free, 1)
                        for ft in range(FT):
                            m = n * FT + ft
                            dve.wait_ge(gelu_f, m + 1)
                            dve.wait_ge(gelu_hi, m + 3)
                            dve.tensor_tensor(glo[ft % 2][:, :], gf[ft % 2][:, :], f32(ghi[ft % 2][:, :]), ALU.subtract).then_inc(g_lo, 1)
                        dve.wait_ge(y_full, n + 1)
                        dve.wait_ge(xs_biased, CT * (n + 1))
                        for tt in range(CT):
                            for half in range(2):
                                m = n * 2 * CT + 2 * tt + half
                                cols = slice(half * HALF, (half + 1) * HALF)
                                dve.tensor_tensor(tmp[:, :], Y[2 * tt + half][:, 0:HALF], gate2[:, cols], ALU.mult).then_inc(y_read, 1)
                                dve.wait_ge(y_read, m + 2)
                                dve.tensor_tensor(xs[:, tt, cols], xs[:, tt, cols], tmp[:, :], ALU.add).then_inc(x2_done, 1)
                                dve.wait_ge(x2_done, m + 1)
                        for f in range(KT + 1):
                            dve.wait_ge(x2T_done, n * (KT + 1) + f + 1)
                            dve.sem_inc(k_free, 1)
                        dve.wait_ge(dz_done, n + 1)
                        dve.sem_inc(k_free, 1)
                        for tt in range(CT):
                            for half in range(2):
                                g = H_OUT + 2 * tt + half
                                cols = slice(half * HALF, (half + 1) * HALF)
                                dve.wait_ge(k_full, n * H_ALL + g + 1)
                                dve.tensor_tensor(xs[:, tt, cols], xs[:, tt, cols], G[(j * H_ALL + g) % 2][:, 0:HALF], ALU.add).then_inc(out_done, 1)
                                dve.wait_ge(out_done, n * 2 * CT + 2 * tt + half + 1)
                                dve.sem_inc(k_free, 1)

            @block.tensor
            def _(pe):
                pe.sem_inc(fc2_mm, 2)
                with pe.Fori(0, BATCH) as b:
                    for j in range(NC):
                        n = b * NC + j

                        def bank(g):
                            pe.wait_ge(k_free, n * H_ALL + g + 1)
                            alone(pe)
                            return G[(j * H_ALL + g) % 2]

                        for f in range(KT + 1):
                            rows = PAR if f < KT else REM
                            to = bank(H_LN + f)
                            for tt in range(CT):
                                if f == 0:
                                    pe.wait_ge(ln2, n * CT + tt + 1)
                                mm = pe.transpose(to[0:rows, tt * PAR:(tt + 1) * PAR], xa[:, tt, f * PAR:f * PAR + rows], ident[:, :])
                            mm.then_inc(k_full, 1)
                        pe.wait_ge(h_split, (n + 1) * (KT + 1) + 2)

                        def fc1(ft):
                            m = n * FT + ft
                            pe.wait_ge(gelu_hi, m + 1)
                            for i, (w, a, rows) in enumerate(PASSES):
                                mm = pe.matmul(F[ft % 2][:, 0:CH], w1[0:rows, w, ft * PAR:(ft + 1) * PAR], h2T[0:rows, a, :],
                                               start=(i == 0), stop=(i == len(PASSES) - 1))
                            mm.then_inc(f_full, 1)

                        def fc2(ft):
                            m = n * FT + ft
                            pe.wait_ge(g_lo, m + 3)
                            for tt in range(CT):
                                span = slice(tt * PAR, (tt + 1) * PAR)
                                for i, (g, w) in enumerate(((ghi, 0), (ghi, 1), (glo, 0))):
                                    for half in range(2):
                                        mm = pe.matmul(Y[2 * tt + half][:, 0:HALF], g[ft % 2][:, span], w2[:, ft, w, half * HALF:(half + 1) * HALF],
                                                       start=(ft == 0 and i == 0), stop=(ft == FT - 1 and i == 2))
                            mm.then_inc(fc2_mm, 1)

                        fc1(0)
                        for ft in range(FT):
                            if ft + 1 < FT:
                                fc1(ft + 1)
                            if ft == 0:
                                pe.wait_ge(y_read, 2 * CT * n + 1)
                            fc2(ft)
                        pe.wait_ge(fc2_mm, (n + 1) * FT + 2)
                        pe.sem_inc(y_full, 1)
                        for f in range(KT + 1):
                            rows = PAR if f < KT else REM
                            to = bank(H_X2 + f)
                            if f == 0:
                                pe.wait_ge(x2_done, 2 * CT * (n + 1))
                            for tt in range(CT):
                                mm = pe.transpose(to[0:rows, tt * PAR:(tt + 1) * PAR], xs[:, tt, f * PAR:f * PAR + rows], ident[:, :])
                            mm.then_inc(k_full, 1)
                        to = bank(H_Z)
                        pe.wait_ge(e_in, 32 * (b + 1))
                        pe.wait_ge(x2T_done, (n + 1) * (KT + 1))
                        for f in range(KT + 1):
                            rows = PAR if f < KT else REM
                            mm = pe.matmul(to[0:RANK, 0:CH], ecur[0:rows, f, :], x2T[0:rows, f, :], start=(f == 0), stop=(f == KT))
                        mm.then_inc(k_full, 1)
                        pe.wait_ge(dz_done, n + 1)
                        for tt in range(CT):
                            for half in range(2):
                                to = bank(H_OUT + 2 * tt + half)
                                pe.matmul(to[:, 0:HALF], dzT[:, tt * PAR:(tt + 1) * PAR], UT[:, half * HALF:(half + 1) * HALF],
                                          start=True, stop=True).then_inc(k_full, 1)


def lay_out(inputs):

    def get(name):
        return np.asarray(inputs[name])

    def tiles(v):
        wide = np.zeros((KT + 1) * PAR, v.dtype)
        wide[:C] = v
        return np.ascontiguousarray(wide.reshape(KT + 1, PAR).T)

    heads = np.arange(C).reshape(HEADS, HD)
    order = np.stack([heads, heads + C], 1).reshape(-1)
    w_qkv, b_qkv = get("L0_cond_W_qkv"), get("L0_cond_b_qkv")
    cond = get("cond_1152")
    cond_t = np.zeros(((KT + 1) * PAR, BATCH), cond.dtype)
    cond_t[:C] = cond.T
    iu, ju = np.triu_indices(RANK, k=1)
    w1, b1 = get("L1_cond_W"), get("L1_cond_b")
    w_rot = np.zeros((C, RANK, RANK), w1.dtype)
    b_rot = np.zeros((RANK, RANK), b1.dtype)
    w_rot[:, iu, ju] = w1.T
    w_rot[:, ju, iu] = w1.T
    b_rot[iu, ju] = b1
    b_rot[ju, iu] = b1
    laid = {
        "x": get("x"), "cond_t": cond_t.reshape(KT + 1, PAR, BATCH),
        "w_ada": get("L0_cond_W_ada"), "b_ada": get("L0_cond_b_ada").reshape(1, -1),
        "w_qk": w_qkv[:, order], "b_qk": b_qkv[order].reshape(QK_TILES, PAR).T,
        "w_v": w_qkv[:, 2 * C:], "b_v": tiles(b_qkv[2 * C:]),
        "w_proj": get("L0_cond_W_proj"), "b_proj": get("L0_cond_b_proj").reshape(1, -1),
        "w_fc1": get("L0_cond_W_fc1"), "b_fc1": get("L0_cond_b_fc1").reshape(FF // PAR, PAR).T,
        "w_fc2": get("L0_cond_W_fc2"), "b_fc2": get("L0_cond_b_fc2").reshape(1, -1),
        "p_cols": get("L1_cond_P"), "p_rows": get("L1_cond_P").T,
        "w_rot": w_rot.reshape(C, RANK * RANK), "b_rot": b_rot.reshape(1, -1),
    }
    return {k: np.ascontiguousarray(v) for k, v in laid.items()}


def declare(nc, laid):
    f = mybir.dt.float32
    aps = {k: nc.dram_tensor(k, v.shape, mybir.dt.from_np(v.dtype), kind="ExternalInput").ap() for k, v in laid.items()}
    for name, shape in (("ada_d", (BATCH, 6 * C)), ("x1_d", (BATCH, TOKENS, C)), ("rot_d", (BATCH, RANK * RANK)),
                        ("e_d", (BATCH, PAR, (KT + 1) * RANK))):
        aps[name] = nc.dram_tensor(name, shape, f).ap()
    aps["out"] = nc.dram_tensor("out", (BATCH, TOKENS, C), f, kind="ExternalOutput").ap()
    build(nc, **aps)


def kernel(**inputs):
    import concourse.bacc as bacc
    from concourse.bass_utils import run_bass_kernel_spmd

    laid = lay_out(inputs)
    nc = bacc.Bacc("TRN2", target_bir_lowering=False, num_devices=1)
    declare(nc, laid)
    r = run_bass_kernel_spmd(nc, [laid], core_ids=[0])
    return r.results[0]["out"]
```
